# Optimizing a Trainium2 kernel written in Bass

```python
import numpy as np
import jax
import jax.numpy as jnp

def _softmax(x, axis=-1):
    return jax.nn.softmax(x, axis=axis)

def _gelu(x):
    return jax.nn.gelu(x, approximate=True)

def _silu(x):
    return jax.nn.silu(x)

def _sigmoid(x):
    return jax.nn.sigmoid(x)

def _layernorm(x, axis=-1, eps=1e-05):
    m = jnp.mean(x, axis=axis, keepdims=True)
    v = jnp.var(x, axis=axis, keepdims=True)
    return (x - m) / jnp.sqrt(v + eps)

def _scatter_add(tgt, idx, src, axis=0):
    return tgt.at[idx].add(src)

def _segment_sum(src, seg, n):
    return jax.ops.segment_sum(src, seg, n)
kernel_name = 'mk_gnn_resnorm_d2_gnn_r8_48f0ff'

def setup_inputs(seed: int=0):
    np.random.seed(seed)
    _w = jnp.asarray

    def _rec_inputs():
        import jax
        import jax.numpy as jnp
        _gk = jax.random.key(seed)
        x = -0.000202 + 1 * jax.random.normal(jax.random.fold_in(_gk, 1), (6250, 128), jnp.float32)
        _s = jax.random.randint(jax.random.fold_in(_gk, 2), (100000,), 0, 6250, jnp.int32)
        _d = jax.random.randint(jax.random.fold_in(_gk, 3), (100000,), 0, 6250, jnp.int32)
        _loop = jnp.arange(6250, dtype=jnp.int32)
        src = jnp.concatenate([_s, _d, _loop])
        dst = jnp.concatenate([_d, _s, _loop])
        _o = jnp.argsort(dst, stable=True)
        src = src[_o]
        dst = dst[_o]
        edge_attr_64 = -7.08334e-05 + 0.999895 * jax.random.normal(jax.random.fold_in(_gk, 12), (206250, 64), jnp.float32)
        return (x, src, dst, edge_attr_64)
    x, src, dst, edge_attr_64 = _rec_inputs()

    def _L0_gnn_setup():
        import jax, jax.numpy as jnp
        import numpy as np
        N_NODES = 6250
        N_EDGES = 75000
        IN_DIM = 128
        EDGE_DIM = 64
        OUT_DIM = 128
        AVG_D_LOG = 2.5
        EPS = 1e-05
        POST_IN = (4 * 3 + 1) * IN_DIM
        key = jax.random.key(seed)
        ks = jax.random.split(key, 10)
        node_feat = jax.random.normal(ks[0], (N_NODES, IN_DIM), dtype=jnp.float32)
        edge_feat = jax.random.normal(ks[1], (N_EDGES, EDGE_DIM), dtype=jnp.float32)
        src = jax.random.randint(ks[2], (N_EDGES,), 0, N_NODES, dtype=jnp.int32)
        dst = jax.random.randint(ks[3], (N_EDGES,), 0, N_NODES, dtype=jnp.int32)
        pre_in = 2 * IN_DIM + EDGE_DIM
        W_pre = jax.random.normal(ks[4], (pre_in, IN_DIM), dtype=jnp.float32) / np.sqrt(pre_in)
        b_pre = jnp.zeros((IN_DIM,), dtype=jnp.float32)
        W_post1 = jax.random.normal(ks[5], (POST_IN, OUT_DIM), dtype=jnp.float32) / np.sqrt(POST_IN)
        b_post1 = jnp.zeros((OUT_DIM,), dtype=jnp.float32)
        W_post2 = jax.random.normal(ks[6], (OUT_DIM, OUT_DIM), dtype=jnp.float32) / np.sqrt(OUT_DIM)
        b_post2 = jnp.zeros((OUT_DIM,), dtype=jnp.float32)
        return {'node_feat': node_feat, 'edge_feat': edge_feat, 'src': src, 'dst': dst, 'W_pre': W_pre, 'b_pre': b_pre, 'W_post1': W_post1, 'b_post1': b_post1, 'W_post2': W_post2, 'b_post2': b_post2}
    _L0_gnn_all = _L0_gnn_setup()
    _L0_gnn_in = {k: v for k, v in _L0_gnn_all.items() if k in ('W_pre', 'b_pre', 'W_post1', 'b_post1', 'W_post2', 'b_post2')}
    del _L0_gnn_all

    def _L1_gnn_setup():
        import jax, jax.numpy as jnp
        import numpy as np
        N = 6250
        IN_DIM = 128
        OUT_DIM = 128
        HEADS = 2
        EPS = 1e-05
        NEG_SLOPE = 0.2

        def _add_self_loops(edge_index, num_nodes):
            loop = jnp.arange(num_nodes, dtype=edge_index.dtype)
            src = jnp.concatenate([edge_index[0], loop])
            dst = jnp.concatenate([edge_index[1], loop])
            return (src, dst)

        def _layernorm(h, gamma, beta):
            mu = jnp.mean(h, axis=-1, keepdims=True)
            var = jnp.mean(jnp.square(h - mu), axis=-1, keepdims=True)
            return (h - mu) * jax.lax.rsqrt(var + EPS) * gamma + beta

        def _silu(h):
            return h * jax.nn.sigmoid(h)

        def _gcn_conv(x, src, dst, W, b, num_nodes):
            h = x @ W
            deg = jnp.zeros((num_nodes,), h.dtype).at[dst].add(1.0)
            dinv = jnp.where(deg > 0, jax.lax.rsqrt(jnp.maximum(deg, 1.0)), 0.0)
            norm = dinv[src] * dinv[dst]
            msg = h[src] * norm[:, None]
            out = jnp.zeros((num_nodes, h.shape[1]), h.dtype).at[dst].add(msg)
            return out + b

        def _gat_conv(x, src, dst, W, att_src, att_dst, b, num_nodes, heads):
            C = W.shape[1] // heads
            h = (x @ W).reshape(num_nodes, heads, C)
            a_src = jnp.sum(h * att_src, axis=-1)
            a_dst = jnp.sum(h * att_dst, axis=-1)
            e = a_src[src] + a_dst[dst]
            e = jnp.where(e > 0, e, NEG_SLOPE * e)
            m = jax.ops.segment_max(e, dst, num_segments=num_nodes)
            ex = jnp.exp(e - m[dst])
            den = jax.ops.segment_sum(ex, dst, num_segments=num_nodes)
            alpha = ex / den[dst]
            msg = h[src] * alpha[:, :, None]
            out = jnp.zeros((num_nodes, heads, C), h.dtype).at[dst].add(msg)
            return jnp.mean(out, axis=1) + b
        key = jax.random.key(seed)
        ks = jax.random.split(key, 9)
        x = jax.random.normal(ks[0], (N, IN_DIM), dtype=jnp.float32)
        edge_index = jax.random.randint(ks[1], (2, 100000), 0, N, dtype=jnp.int64)
        s = 1.0 / np.sqrt(IN_DIM)
        gcn_w = jax.random.uniform(ks[2], (IN_DIM, OUT_DIM), jnp.float32, -s, s)
        gcn_b = jnp.zeros((OUT_DIM,), jnp.float32)
        so = 1.0 / np.sqrt(OUT_DIM)
        gat_w = jax.random.uniform(ks[3], (OUT_DIM, HEADS * OUT_DIM), jnp.float32, -so, so)
        att_src = jax.random.uniform(ks[4], (HEADS, OUT_DIM), jnp.float32, -so, so)
        att_dst = jax.random.uniform(ks[5], (HEADS, OUT_DIM), jnp.float32, -so, so)
        gat_b = jnp.zeros((OUT_DIM,), jnp.float32)
        ln_gamma = jnp.ones((OUT_DIM,), jnp.float32)
        ln_beta = jnp.zeros((OUT_DIM,), jnp.float32)
        return dict(x=x, edge_index=edge_index, gcn_w=gcn_w, gcn_b=gcn_b, gat_w=gat_w, att_src=att_src, att_dst=att_dst, gat_b=gat_b, ln_gamma=ln_gamma, ln_beta=ln_beta)
    _L1_gnn_all = _L1_gnn_setup()
    _L1_gnn_in = {k: v for k, v in _L1_gnn_all.items() if k in ('gcn_w', 'gcn_b', 'gat_w', 'att_src', 'att_dst', 'gat_b', 'ln_gamma', 'ln_beta')}
    del _L1_gnn_all
    return {'x': x, 'src': src, 'dst': dst, 'edge_attr_64': edge_attr_64, 'L0_gnn_W_pre': _L0_gnn_in['W_pre'], 'L0_gnn_b_pre': _L0_gnn_in['b_pre'], 'L0_gnn_W_post1': _L0_gnn_in['W_post1'], 'L0_gnn_b_post1': _L0_gnn_in['b_post1'], 'L0_gnn_W_post2': _L0_gnn_in['W_post2'], 'L0_gnn_b_post2': _L0_gnn_in['b_post2'], 'L1_gnn_gcn_w': _L1_gnn_in['gcn_w'], 'L1_gnn_gcn_b': _L1_gnn_in['gcn_b'], 'L1_gnn_gat_w': _L1_gnn_in['gat_w'], 'L1_gnn_att_src': _L1_gnn_in['att_src'], 'L1_gnn_att_dst': _L1_gnn_in['att_dst'], 'L1_gnn_gat_b': _L1_gnn_in['gat_b'], 'L1_gnn_ln_gamma': _L1_gnn_in['ln_gamma'], 'L1_gnn_ln_beta': _L1_gnn_in['ln_beta']}

def reference(x, src, dst, edge_attr_64, L0_gnn_W_pre, L0_gnn_b_pre, L0_gnn_W_post1, L0_gnn_b_post1, L0_gnn_W_post2, L0_gnn_b_post2, L1_gnn_gcn_w, L1_gnn_gcn_b, L1_gnn_gat_w, L1_gnn_att_src, L1_gnn_att_dst, L1_gnn_gat_b, L1_gnn_ln_gamma, L1_gnn_ln_beta):
    import jax
    import jax.numpy as jnp

    def _L0_gnn_ref(node_feat, edge_feat, src, dst, W_pre, b_pre, W_post1, b_post1, W_post2, b_post2):
        import jax, jax.numpy as jnp
        import numpy as np
        N_NODES = 6250
        N_EDGES = 75000
        IN_DIM = 128
        EDGE_DIM = 64
        OUT_DIM = 128
        AVG_D_LOG = 2.5
        EPS = 1e-05
        POST_IN = (4 * 3 + 1) * IN_DIM
        N = node_feat.shape[0]
        z2 = jnp.concatenate([node_feat[src], node_feat[dst], edge_feat], axis=-1)
        e = jax.nn.relu(z2 @ W_pre + b_pre)
        deg = jax.ops.segment_sum(jnp.ones((e.shape[0],), e.dtype), dst, num_segments=N)
        safe_deg = jnp.maximum(deg, 1.0)[:, None]
        s = jax.ops.segment_sum(e, dst, num_segments=N)
        mean = s / safe_deg
        mean_sq = jax.ops.segment_sum(e * e, dst, num_segments=N) / safe_deg
        var = jax.nn.relu(mean_sq - mean * mean)
        std = jnp.sqrt(var + EPS)
        mx = jax.ops.segment_max(e, dst, num_segments=N)
        mn = jax.ops.segment_min(e, dst, num_segments=N)
        has_edges = (deg > 0)[:, None]
        mean = jnp.where(has_edges, mean, 0.0)
        mx = jnp.where(has_edges, mx, 0.0)
        mn = jnp.where(has_edges, mn, 0.0)
        std = jnp.where(has_edges, std, 0.0)
        agg = jnp.concatenate([mean, mx, mn, std], axis=-1)
        logd = jnp.log(deg + 1.0)[:, None]
        amp = agg * (logd / AVG_D_LOG)
        att = agg * jnp.where(deg[:, None] > 0, AVG_D_LOG / jnp.maximum(logd, EPS), 0.0)
        h_agg = jnp.concatenate([agg, amp, att], axis=-1)
        h = jnp.concatenate([node_feat, h_agg], axis=-1)
        h = jax.nn.relu(h @ W_post1 + b_post1)
        h = h @ W_post2 + b_post2
        return h + node_feat

    def _L1_gnn_ref(x, edge_index, gcn_w, gcn_b, gat_w, att_src, att_dst, gat_b, ln_gamma, ln_beta):
        import jax, jax.numpy as jnp
        import numpy as np
        N = 6250
        IN_DIM = 128
        OUT_DIM = 128
        HEADS = 2
        EPS = 1e-05
        NEG_SLOPE = 0.2

        def _add_self_loops(edge_index, num_nodes):
            loop = jnp.arange(num_nodes, dtype=edge_index.dtype)
            src = jnp.concatenate([edge_index[0], loop])
            dst = jnp.concatenate([edge_index[1], loop])
            return (src, dst)

        def _layernorm(h, gamma, beta):
            mu = jnp.mean(h, axis=-1, keepdims=True)
            var = jnp.mean(jnp.square(h - mu), axis=-1, keepdims=True)
            return (h - mu) * jax.lax.rsqrt(var + EPS) * gamma + beta

        def _silu(h):
            return h * jax.nn.sigmoid(h)

        def _gcn_conv(x, src, dst, W, b, num_nodes):
            h = x @ W
            deg = jnp.zeros((num_nodes,), h.dtype).at[dst].add(1.0)
            dinv = jnp.where(deg > 0, jax.lax.rsqrt(jnp.maximum(deg, 1.0)), 0.0)
            norm = dinv[src] * dinv[dst]
            msg = h[src] * norm[:, None]
            out = jnp.zeros((num_nodes, h.shape[1]), h.dtype).at[dst].add(msg)
            return out + b

        def _gat_conv(x, src, dst, W, att_src, att_dst, b, num_nodes, heads):
            C = W.shape[1] // heads
            h = (x @ W).reshape(num_nodes, heads, C)
            a_src = jnp.sum(h * att_src, axis=-1)
            a_dst = jnp.sum(h * att_dst, axis=-1)
            e = a_src[src] + a_dst[dst]
            e = jnp.where(e > 0, e, NEG_SLOPE * e)
            m = jax.ops.segment_max(e, dst, num_segments=num_nodes)
            ex = jnp.exp(e - m[dst])
            den = jax.ops.segment_sum(ex, dst, num_segments=num_nodes)
            alpha = ex / den[dst]
            msg = h[src] * alpha[:, :, None]
            out = jnp.zeros((num_nodes, heads, C), h.dtype).at[dst].add(msg)
            return jnp.mean(out, axis=1) + b
        num_nodes = x.shape[0]
        src, dst = _add_self_loops(edge_index, num_nodes)
        h = _gcn_conv(x, src, dst, gcn_w, gcn_b, num_nodes)
        h = _silu(_layernorm(h, ln_gamma, ln_beta))
        h = _gat_conv(h, src, dst, gat_w, att_src, att_dst, gat_b, num_nodes, HEADS)
        h = _silu(_layernorm(h, ln_gamma, ln_beta))
        return h
    edge_index = jnp.stack([src, dst])
    x = _layernorm(x + _L0_gnn_ref(x, edge_attr_64, src, dst, L0_gnn_W_pre, L0_gnn_b_pre, L0_gnn_W_post1, L0_gnn_b_post1, L0_gnn_W_post2, L0_gnn_b_post2), axis=-1)
    x = _layernorm(x + _L1_gnn_ref(x, edge_index, L1_gnn_gcn_w, L1_gnn_gcn_b, L1_gnn_gat_w, L1_gnn_att_src, L1_gnn_att_dst, L1_gnn_gat_b, L1_gnn_ln_gamma, L1_gnn_ln_beta), axis=-1)
    return x

_drawn_inputs = setup_inputs


def setup_inputs(seed=0):
    import zlib

    import numpy as np

    out = dict(_drawn_inputs(seed))
    spreads = {'L0_gnn_b_pre': (0.0, 0.1),
     'L0_gnn_b_post1': (0.0, 0.1),
     'L0_gnn_b_post2': (0.0, 0.1),
     'L1_gnn_gcn_b': (0.0, 0.1),
     'L1_gnn_gat_b': (0.0, 0.1),
     'L1_gnn_ln_gamma': (1.0, 0.2),
     'L1_gnn_ln_beta': (0.0, 0.1)}
    factors = {'L1_gnn_att_src': 8.0, 'L1_gnn_att_dst': 8.0}
    for name, (base, spread) in spreads.items():
        noise = np.random.default_rng([zlib.crc32(name.encode()), seed]).standard_normal(out[name].shape)
        drawn = base * np.exp(spread * noise) if base else spread * noise
        out[name] = jnp.asarray(drawn.astype(out[name].dtype))
    for name, factor in factors.items():
        out[name] = (out[name] * factor).astype(out[name].dtype)
    return out
```

```python
from contextlib import ExitStack

import concourse.bass as bass
from concourse import mybir

F32 = mybir.dt.float32
BF16 = mybir.dt.bfloat16
I32 = mybir.dt.int32
ALU = mybir.AluOpType
ACT = mybir.ActivationFunctionType
ds = bass.ds

N = 6250
E = 206250
NP = 6400
NB = NP // 128
CH = 512
NCH = (E + CH - 1) // CH
EP = NCH * CH
COLS = EP // 128
W = 64
TMAX = 512
TK = 2 * TMAX + 24
TLESS = 64
BIG = 1.0e30
EPS = 1e-5
GROUPS = [(g * 512, min(512, NP - g * 512)) for g in range((NP + 511) // 512)]


class Entry:

    def __init__(self, i, o):
        self.i, self.o = i, o

    def at(self, n=0):
        return self.i + (self.o + n)

    def slot(self, m):
        return self.o % m

    def uses(self, m, n=0):
        return (self.i + (self.o + m * (1 + n))) // m

    def first(self, m):
        return isinstance(self.i, int) and self.i + self.o < m


def pipeline(eng, T, U, D, stages):
    for i in range(D):
        for lag, f in stages:
            if i >= lag:
                f(Entry(i // U * U, i % U - lag))
    with eng.bass.Fori(D, T, U, engines=bass.OrderedEngineSet([eng.engine])) as i:
        for k in range(U):
            for lag, f in stages:
                f(Entry(i, k - lag))
    for k in range(D):
        for lag, f in stages:
            if k < lag:
                f(Entry(T, k - lag))


class Chain:

    def __init__(self, eng, sem):
        self.eng, self.sem, self.n = eng, sem, 0

    def __call__(self, ins):
        self.n += 1
        return ins.then_inc(self.sem, 1)

    def sync(self):
        self.eng.wait_ge(self.sem, self.n)

    def raises(self, sem):
        self.sync()
        self.eng.engine_nop().then_inc(sem, 1)


def build(nc, d, out, upto=99):
    with ExitStack() as top:
        def sem(name):
            return top.enter_context(nc.semaphore(name))

        def sbt(stack, name, shape, dt=F32):
            return stack.enter_context(nc.sbuf_tensor(name, shape, dt))

        def pst(stack, name, shape, dt=F32):
            return stack.enter_context(nc.psum_tensor(name, shape, dt))

        def dram(name, shape, dt=F32):
            return nc.dram_tensor(name, shape, dt).ap()

        Atab = dram("Atab", [NP, 128])
        Btab = dram("Btab", [NP, 128])
        MM = dram("MM", [2, EP], BF16)
        TBI = dram("TBI", [2 * TMAX], I32)
        TBF = dram("TBF", [TMAX], F32)
        X1D = dram("X1D", [NP, 128])
        XS = dram("XS", [NP, 128])
        TAB = dram("TAB", [NP, 130])
        ADT = dram("ADT", [NP, 2])
        DQ = dram("DQ", [3, NP])

        acc = sbt(top, "acc", [128, 5, NP])
        baseF = sbt(top, "baseF", [128, TMAX + 16])
        tb = sbt(top, "tb", [1, 2 * TMAX + 32], I32)
        ident = sbt(top, "ident", [128, 128])
        iotaW = sbt(top, "iotaW", [128, W])
        nid = sbt(top, "nid", [128, 1])
        ones = sbt(top, "ones", [128, 128])
        dinv = sbt(top, "dinv", [128, NB])
        onesb = sbt(top, "onesb", [128, 128], BF16)

        s_pool = sem("s_pool")
        s_sync = sem("s_sync")
        s_pad = sem("s_pad")

        with ExitStack() as ph:
            xT = acc[:, 0, :]
            wsd = sbt(ph, "wsd", [128, 2, 128])
            bpre = sbt(ph, "bpre", [1, 128])
            stg = sbt(ph, "stg", [128, 2, 5, 256])
            dn = sbt(ph, "dn", [128, COLS], I32)
            dp = sbt(ph, "dp", [128, COLS], I32)
            mk = sbt(ph, "mk", [128, COLS], BF16)
            mk2 = sbt(ph, "mk2", [128, COLS], BF16)
            rows = sbt(ph, "rows", [1, 8, NCH + 1])
            rowi = sbt(ph, "rowi", [1, 2, NCH + 1], I32)
            ob = sbt(ph, "ob", [128, 2, NCH])
            iotaC = sbt(ph, "iotaC", [128, NCH])
            tcol = sbt(ph, "tcol", [128, 4])
            tmp = sbt(ph, "tmp", [128, 2, NCH])
            cols = sbt(ph, "cols", [128, 6])
            tabf = sbt(ph, "tabf", [128, 2, 4])
            tabi = sbt(ph, "tabi", [128, 2, 4], I32)
            pw = [pst(ph, f"pw{k}", [128, 512]) for k in range(4)]
            pb = [pst(ph, f"pb{k}", [128, 512]) for k in range(2)]
            p_in = sem("p_in")
            p_idx = sem("p_idx")
            p_row = sem("p_row")
            p_c = sem("p_c")
            p_mm = sem("p_mm")
            p_ev = sem("p_ev")
            p_x = [sem("p_x0"), sem("p_x1")]
            p_z = sem("p_z")
            p_out = [sem("p_out0"), sem("p_out1")]
            p_d = sem("p_d")
            p_bc = sem("p_bc")
            p_rw = sem("p_rw")
            p_msk = sem("p_msk")
            p_tab = sem("p_tab")
            p_fin = sem("p_fin")
            blk = ph.enter_context(nc.Block())

            @blk.sync
            def _(e):
                e.dma_start(wsd[:, 0, :], d["wpre"][0:128, :]).then_inc(p_in, 16)
                e.dma_start(wsd[:, 1, :], d["wpre"][128:256, :]).then_inc(p_in, 16)
                e.dma_start(bpre[0:1, :], d["bpre"].rearrange("(a n) -> a n", a=1)).then_inc(p_in, 16)
                for k in range(2):
                    c = slice(k * NP // 2, (k + 1) * NP // 2)
                    e.dma_start(xT[:, c], d["xT"][:, c]).then_inc(p_x[k], 16)
                for g in range(NB // 5):
                    e.wait_ge(p_ev, 5 * (g + 1))
                    for t, o in ((Atab, 0), (Btab, 128)):
                        e.dma_start(t[g * 640:(g + 1) * 640, :].rearrange("(b p) f -> p b f", p=128),
                                    stg[:, g % 2, :, o:o + 128]).then_inc(p_out[g % 2], 16)
                e.wait_ge(p_out[0], 16 * 2 * 5)
                e.wait_ge(p_out[1], 16 * 2 * 5)

            @blk.gpsimd
            def _(e):
                e.memset(ident[:, :], 0.0).then_inc(p_c, 1)
                e.wait_ge(p_c, 1)
                e.affine_select(out=ident[:, :], in_=ident[:, :], compare_op=ALU.not_equal, fill=1.0,
                                base=0, pattern=[[-1, 128]], channel_multiplier=1).then_inc(p_c, 1)
                e.memset(ones[:, :], 1.0).then_inc(p_c, 1)
                e.memset(onesb[:, :], 1.0).then_inc(p_c, 1)
                e.iota(iotaW[:, :], pattern=[[1, W]], base=0, channel_multiplier=0,
                       allow_small_or_imprecise_dtypes=True).then_inc(p_c, 1)
                e.iota(cols[:, 5:6], pattern=[[0, 1]], base=0, channel_multiplier=1,
                       allow_small_or_imprecise_dtypes=True).then_inc(p_c, 1)
                e.iota(iotaC[:, :], pattern=[[1, NCH]], base=0, channel_multiplier=0,
                       allow_small_or_imprecise_dtypes=True).then_inc(p_c, 1)
                e.iota(tcol[:, :], pattern=[[128, 4]], base=0, channel_multiplier=1,
                       allow_small_or_imprecise_dtypes=True).then_inc(p_c, 1)
                e.memset(acc[:, 1:5, :], 0.0).then_inc(p_z, 1)
                e.wait_ge(p_msk, 2)
                e.dma_start(MM[0, :].rearrange("(p t) -> p t", p=128), mk[:, :]).then_inc(p_fin, 16)
                e.dma_start(MM[1, :].rearrange("(p t) -> p t", p=128), mk2[:, :]).then_inc(p_fin, 16)
                e.wait_ge(p_tab, 2)
                e.dma_start(TBI.rearrange("(k j p) -> p k j", k=2, p=128), tabi[:, :, :], allow_slow_non_contiguous=True).then_inc(p_fin, 16)
                e.dma_start(TBF.rearrange("(j p) -> p j", p=128), tabf[:, 1, :], allow_slow_non_contiguous=True).then_inc(p_fin, 16)
                e.wait_ge(p_fin, 64)
                e.dma_start(tb[0:1, 0:2 * TMAX], TBI.rearrange("(a n) -> a n", a=1)).then_inc(p_fin, 16)
                e.dma_start(baseF[:, 0:TMAX], TBF.partition_broadcast(128)).then_inc(p_fin, 16)
                e.wait_ge(p_fin, 96)

            @blk.tensor
            def _(e):
                e.wait_ge(p_in, 48)
                e.wait_ge(p_c, 3)
                for b in range(NB):
                    e.wait_ge(p_x[2 * b // NB], 16)
                    if b >= 4:
                        e.wait_ge(p_ev, b - 3)
                    t = pw[b % 4]
                    xb = xT[:, b * 128:(b + 1) * 128]
                    e.matmul(t[:, 0:128], xb, wsd[:, 0, :], start=True, stop=True)
                    e.matmul(t[:, 128:256], xb, wsd[:, 1, :], start=True, stop=False)
                    e.matmul(t[:, 128:256], ones[0:1, :], bpre[0:1, :], start=False, stop=True).then_inc(p_mm, 1)
                    if b == 0:
                        e.wait_ge(p_rw, 1)
                        for k in range(2):
                            e.matmul(pb[k][:, 0:NCH], ones[0:1, :], rows[0:1, k, 0:NCH],
                                     start=True, stop=True).then_inc(p_bc, 1)

            @blk.scalar
            def _(e):
                for k in range(2):
                    e.dma_start(rowi[0:1, k, 0:NCH],
                                d["lin"][1:1 + EP].rearrange("(a c b) -> a c b", a=1, b=CH)[:, :, k * (CH - 1)],
                                allow_slow_non_contiguous=True).then_inc(p_row, 16)
                e.dma_start(dn[:, :], d["lin"][1:1 + EP].rearrange("(p t) -> p t", p=128)).then_inc(p_idx, 16)
                e.dma_start(dp[:, :], d["lin"][0:EP].rearrange("(p t) -> p t", p=128)).then_inc(p_idx, 16)
                for b in range(NB):
                    g = b // 5
                    e.wait_ge(p_mm, b + 1)
                    if b % 5 == 0 and g >= 2:
                        e.wait_ge(p_out[g % 2], 32 * (g // 2))
                    e.copy(stg[:, g % 2, b % 5, :], pw[b % 4][:, 0:256]).then_inc(p_ev, 1)

            @blk.vector
            def _(e):
                ch = Chain(e, p_d)
                R = lambda k: rows[0:1, k, 0:NCH]
                e.wait_ge(p_row, 32)
                ch(e.tensor_copy(R(1), rowi[0:1, 0, 0:NCH]))
                ch(e.tensor_copy(R(2), rowi[0:1, 1, 0:NCH]))
                ch(e.memset(R(6), 1.0))
                ch.sync()
                ch(e.tensor_tensor(rowi[0:1, 0, 0:NCH], R(2), R(1), ALU.subtract))
                ch.sync()
                ch(e.tensor_scalar(rowi[0:1, 1, 0:NCH], rowi[0:1, 0, 0:NCH], 6, None, ALU.arith_shift_right))
                ch.sync()
                ch(e.tensor_scalar(R(4), rowi[0:1, 1, 0:NCH], 1.0, None, ALU.add))
                ch.sync()
                ch(e.tensor_tensor_scan(R(5), R(6), R(4), 0.0, ALU.mult, ALU.add))
                ch.sync()
                ch(e.tensor_tensor(R(0), R(5), R(4), ALU.subtract))
                ch.sync()
                for k, m in ((0, 2), (1, 3)):
                    o = rowi[0:1, 0, k:k + 1]
                    ch(e.tensor_scalar(o, rows[0:1, 5, NCH - 1:NCH], float(2 ** m - 1), None, ALU.add))
                    ch.sync()
                    ch(e.tensor_scalar(o, o, m, m, ALU.arith_shift_right, ALU.arith_shift_left))
                    ch.sync()
                    ch(e.tensor_scalar(tb[0:1, TK + k:TK + k + 1], o, float(-TLESS), None, ALU.add))
                ch.sync()
                e.engine_nop().then_inc(p_rw, 1)
                e.wait_ge(p_bc, 2)
                e.wait_ge(p_c, 8)
                ch(e.tensor_scalar(cols[:, 4:5], cols[:, 5:6], float(W), float(-W), ALU.is_ge, ALU.mult))
                ch.sync()
                ch(e.tensor_tensor(nid[:, :], cols[:, 5:6], cols[:, 4:5], ALU.add))
                ch(e.tensor_copy(ob[:, 0, :], pb[0][:, 0:NCH]))
                ch(e.tensor_copy(ob[:, 1, :], pb[1][:, 0:NCH]))
                ch.sync()
                for j in range(4):
                    t = tcol[:, j:j + 1]
                    ch(e.tensor_scalar(tmp[:, 0, :], ob[:, 0, :], t, None, ALU.is_le))
                    ch.sync()
                    ch(e.tensor_reduce(cols[:, 0:1], tmp[:, 0, :], mybir.AxisListType.X, ALU.add))
                    ch.sync()
                    ch(e.tensor_scalar(tabf[:, 0, j:j + 1], cols[:, 0:1], -1.0, None, ALU.add))
                    ch.sync()
                    ch(e.tensor_scalar(tmp[:, 0, :], iotaC[:, :], tabf[:, 0, j:j + 1], None, ALU.is_equal))
                    ch.sync()
                    for k in range(2):
                        ch(e.tensor_tensor(tmp[:, 1, :], tmp[:, 0, :], ob[:, k, :], ALU.mult))
                        ch.sync()
                        ch(e.tensor_reduce(cols[:, 1 + k:2 + k], tmp[:, 1, :], mybir.AxisListType.X, ALU.add))
                        ch.sync()
                    ch(e.tensor_tensor(cols[:, 3:4], t, cols[:, 1:2], ALU.subtract))
                    ch.sync()
                    ch(e.tensor_scalar(cols[:, 4:5], cols[:, 3:4], float(W), cols[:, 2:3], ALU.mult, ALU.add))
                    ch.sync()
                    ch(e.tensor_scalar(tabf[:, 1, j:j + 1], cols[:, 4:5], float(N), None, ALU.min))
                    ch.sync()
                e.tensor_copy(tabi[:, :, :], tabf[:, :, :]).then_inc(p_tab, 1)
                e.engine_nop().then_inc(p_tab, 1)
                e.wait_ge(p_idx, 32)
                e.tensor_tensor(mk[:, :], dn[:, :], dp[:, :], ALU.is_equal).then_inc(p_msk, 1)
                ch(e.tensor_tensor(mk2[:, :], dn[:, :], dp[:, :], ALU.not_equal))
                ch.sync()
                e.tensor_scalar(mk2[:, :], mk2[:, :], BIG, None, ALU.mult).then_inc(p_msk, 1)
                for b in range(0, NB, 10):
                    e.wait_ge(p_mm, b + 10)
                    ch(e.memset(acc[:, 0, b * 128:(b + 10) * 128], 0.0))
                ch.sync()
                e.wait_ge(p_z, 1)
        if upto < 1:
            return
        phase_l0(nc, d, locals())
        if upto < 2:
            return
        phase_n1(nc, d, locals())
        if upto < 3:
            return
        phase_gcn(nc, d, locals())
        if upto < 4:
            return
        phase_n2(nc, d, locals())
        if upto < 5:
            return
        phase_gat(nc, d, locals())
        phase_n3(nc, d, locals(), out)


def wait(e, s, v):
    if not isinstance(v, int) or v > 0:
        e.wait_ge(s, v)


def keep(e, regs, j, b):
    e.reg_mov(regs[j.slot(len(regs))], b)
    return b


def kept(e, regs, j):
    return e.snap(regs[j.slot(len(regs))], min_val=0, max_val=N)


def wait_sync(e, s, v, pad):
    e.wait_ge(s, v)
    e.sem_inc(pad, 1)


def load_T(e, tb, k):
    return e.value_load(tb[0:1, TK + k:TK + k + 1], min_val=NCH - TLESS, max_val=TMAX - TLESS) + TLESS


def chunk_of(e, tb, j):
    return e.value_load(tb[0:1, ds(j.at(), 1)], min_val=0, max_val=NCH - 1)


def base_of(e, tb, j):
    return e.value_load(tb[0:1, ds(j.at() + TMAX, 1)], min_val=0, max_val=N)


def phase_l0(nc, d, v):
    sem, sbt, pst = v["sem"], v["sbt"], v["pst"]
    acc, baseF, tb = v["acc"], v["baseF"], v["tb"]
    ident, iotaW, nid, onesb = v["ident"], v["iotaW"], v["nid"], v["onesb"]
    Atab, Btab, MM = v["Atab"], v["Btab"], v["MM"]
    with ExitStack() as ph:
        meta = sbt(ph, "meta", [128, 4, 12], I32)
        ZR = sbt(ph, "ZR", [128, 4, CH])
        WB = sbt(ph, "WB", [128, 4, 128])
        dstb = sbt(ph, "dstb", [128, 4, CH], I32)
        mm2 = sbt(ph, "mm2", [128, 4, 2, CH], BF16)
        G = sbt(ph, "G", [128, 4, 4, 128])
        EE = sbt(ph, "EE", [128, 2, 2, CH])
        oh = sbt(ph, "oh", [128, 4, 4, W])
        ohb = sbt(ph, "ohb", [128, 2, 4, W], BF16)
        ohl = sbt(ph, "ohl", [128, 4, 4, W])
        neq = sbt(ph, "neq", [128, 4, 4])
        iob = sbt(ph, "iob", [128, 2, W])
        ST = sbt(ph, "ST", [128, 2, 2, CH])
        BS = sbt(ph, "BS", [128, 2, 2, CH])
        Z = [pst(ph, f"Z{k}", [128, CH]) for k in range(2)]
        ET = [pst(ph, f"ET{k}", [128, CH]) for k in range(2)]
        S1 = pst(ph, "S1", [128, 512])
        S2 = pst(ph, "S2", [128, 512])
        BK = [pst(ph, f"BK{k}", [128, CH]) for k in range(2)]
        S1v = S1[:, 0:3 * W].rearrange("p (a n) -> p a n", a=3)
        S2v = S2[:, 0:2 * W].rearrange("p (a n) -> p a n", a=2)
        l_we = sem("l_we")
        l_mt = [sem(f"l_mt{k}") for k in range(4)]
        l_in = [sem(f"l_in{k}") for k in range(4)]
        l_db = [sem(f"l_db{k}") for k in range(4)]
        l_m = [sem(f"l_m{k}") for k in range(4)]
        l_g = [sem(f"l_g{k}") for k in range(4)]
        s_iob = sem("l_iob")
        s_zr = sem("l_zr")
        s_d1 = sem("l_d1")
        s_p1 = sem("l_p1")
        s_d2 = sem("l_d2")
        s_r = sem("l_r")
        s_a1 = sem("l_a1")
        s_p2 = sem("l_p2")
        s_p2t = sem("l_p2t")
        s_d3 = sem("l_d3")
        s_ohl = sem("l_ohl")
        s_p3 = sem("l_p3")
        s_a2 = sem("l_a2")
        s_p4 = sem("l_p4")
        s_d4a = sem("l_d4a")
        s_d4b = sem("l_d4b")
        s_i = sem("l_i")
        s_pool = v["s_pool"]
        s_pad = v["s_pad"]
        s_sync = v["s_sync"]
        blk = ph.enter_context(nc.Block())
        U, D = 4, 8

        @blk.sync
        def _(e):
            for k in range(4):
                e.dma_start(WB[0:64, k, :], d["wpre"][256:320, :]).then_inc(l_we, 16)
            T = load_T(e, tb, 0)

            def loads(j):
                c, b = chunk_of(e, tb, j), base_of(e, tb, j)
                k = j.slot(4)
                e0 = c * CH
                src = (d["meta"][ds(c, 1), :, :].rearrange("a p s -> (a p) s"), d["eft"][:, ds(e0, CH)],
                       Btab[ds(b, 64), :], d["lin"][ds(e0 + 1, CH)].partition_broadcast(64))
                before = 64 * j.uses(4, -1), j.at(-3)
                if not j.first(4):
                    wait_sync(e, l_g[k], before[0], s_sync)
                    wait_sync(e, s_d1, before[1], s_sync)
                e.dma_start(meta[:, k, :], src[0]).then_inc(l_mt[k], 16)
                if not j.first(4):
                    wait_sync(e, s_p1, before[1], s_sync)
                e.dma_start(ZR[0:64, k, :], src[1]).then_inc(l_in[k], 16)
                e.dma_start(WB[64:128, k, :], src[2]).then_inc(l_in[k], 16)
                e.dma_start(dstb[64:128, k, :], src[3]).then_inc(l_db[k], 16)

            pipeline(e, T, U, D, [(0, loads)])

        @blk.gpsimd
        def _(e):
            T = load_T(e, tb, 0)

            def gather(j):
                k = j.slot(4)
                wait(e, l_mt[k], 16 * j.uses(4))
                if not j.first(4):
                    wait(e, s_d2, j.at(-3))
                e.sem_inc(s_pool, 1)
                for s in range(4):
                    e.indirect_dma_start(G[:, k, s, :], None, Atab,
                                         bass.IndirectOffsetOnAxis(ap=meta[:, k, s:s + 1], axis=0)).then_inc(l_g[k], 16)

            pipeline(e, T, U, D, [(0, gather)])

        @blk.vector
        def _(e):
            e.memset(ST[:, :, :, :], 0.0).then_inc(s_i, 1)
            e.wait_ge(s_i, 1)
            T = load_T(e, tb, 0)

            def d1(j):
                k, q = j.slot(4), j.slot(2)
                e.tensor_scalar(iob[:, q, :], iotaW[:, :], baseF[:, ds(j.at(), 1)], None, ALU.add).then_inc(s_iob, 1)
                wait(e, l_db[k], 16 * j.uses(4))
                if not j.first(4):
                    wait(e, s_p1, j.at(-3))
                e.tensor_scalar(ZR[64:128, k, :], dstb[64:128, k, :], baseF[64:128, ds(j.at(), 1)], nid[64:128, 0:1],
                                ALU.subtract, ALU.is_equal).then_inc(s_zr, 1)
                wait(e, l_mt[k], 16 * j.uses(4))
                if not j.first(4):
                    wait(e, s_ohl, j.at(-3))
                e.tensor_tensor(neq[:, k, :], meta[:, k, 4:8], meta[:, k, 8:12], ALU.not_equal)
                if not j.first(4):
                    wait(e, s_p2, j.at(-3))
                wait(e, s_iob, j.at(1))
                e.tensor_tensor(oh[:, k, :, :], iob[:, q:q + 1, :].to_broadcast([128, 4, W]),
                                meta[:, k, 4:8].unsqueeze(2).to_broadcast([128, 4, W]),
                                ALU.is_equal).then_inc(s_d1, 1)

            def d2(j):
                wait(e, s_p1, j.at(1))
                wait(e, l_g[j.slot(4)], 64 * j.uses(4))
                if not j.first(2):
                    wait(e, s_p2, j.at(-1))
                e.tensor_tensor(EE[:, j.slot(2), 1, :], Z[j.slot(2)][:, :],
                                G[:, j.slot(4), :, :].rearrange("p s f -> p (s f)"), ALU.add).then_inc(s_d2, 1)

            def last(j):
                k = j.slot(4)
                if not j.first(4):
                    wait(e, s_p4, j.at(-3))
                wait(e, s_d1, j.at(1))
                e.tensor_tensor(ohl[:, k, :, :], oh[:, k, :, :], neq[:, k, :].unsqueeze(2).to_broadcast([128, 4, W]),
                                ALU.mult).then_inc(s_ohl, 1)

            def d3(j):
                k, q = j.slot(4), j.slot(2)
                wait(e, s_p2t, j.at(1))
                wait(e, l_m[k], 16 * j.uses(4))
                if not j.first(2):
                    wait(e, s_p3, j.at(-1))
                if not j.first(1):
                    wait(e, s_d3, j.at())
                e.tensor_tensor_scan(ST[:, q, 0, :], mm2[:, k, 0, :], ET[q][:, :], ST[:, 1 - q, 0, CH - 1:CH],
                                     ALU.mult, ALU.max)
                e.tensor_tensor_scan(ST[:, q, 1, :], mm2[:, k, 1, :], ET[q][:, :], ST[:, 1 - q, 1, CH - 1:CH],
                                     ALU.max, ALU.min).then_inc(s_d3, 1)

            def d4(j, S, n, lo, s_in, s_out):
                b = base_of(e, tb, j)
                wait(e, s_in, j.at(1))
                if not j.first(1):
                    wait(e, s_out, j.at())
                a = acc[:, lo:lo + n, ds(b, W)]
                e.tensor_tensor(a, a, S, ALU.add).then_inc(s_out, 1)

            def d4a(j):
                d4(j, S1v, 3, 0, s_p2, s_d4a)

            def d4b(j):
                d4(j, S2v, 2, 3, s_p4, s_d4b)

            pipeline(e, T, U, D, [(7, d4b), (2, d2), (0, d1), (3, last), (4, d4a), (4, d3)])

        @blk.scalar
        def _(e):
            T = load_T(e, tb, 0)

            def a1(j):
                q = j.slot(2)
                wait(e, s_d1, j.at(1))
                if not j.first(2):
                    wait(e, s_p2, j.at(-1))
                e.copy(ohb[:, q, :, :], oh[:, j.slot(4), :, :])
                wait(e, s_d2, j.at(1))
                e.activation(EE[:, q, 0, :], EE[:, q, 1, :], ACT.Relu).then_inc(s_r, 1)
                wait(e, s_r, j.at(1))
                e.activation(EE[:, q, 1, :], EE[:, q, 0, :], ACT.Square).then_inc(s_a1, 1)

            def masks(j):
                c = chunk_of(e, tb, j)
                k = j.slot(4)
                if not j.first(4):
                    wait(e, s_d3, j.at(-3))
                    e.sem_inc(s_pad, 1)
                e.dma_start(mm2[:, k, :, :], MM[:, ds(c * CH, CH)].partition_broadcast(128)).then_inc(l_m[k], 16)

            def a2(j):
                q = j.slot(2)
                wait(e, s_p3, j.at(1))
                if not j.first(2):
                    wait(e, s_p4, j.at(-1))
                e.copy(BS[:, q, 0, :], BK[0][:, :])
                e.copy(BS[:, q, 1, :], BK[1][:, :]).then_inc(s_a2, 1)

            pipeline(e, T, U, D, [(5, a2), (1, masks), (2, a1)])

        @blk.tensor
        def _(e):
            e.wait_ge(l_we, 64)
            T = load_T(e, tb, 0)

            def p1(j):
                q, k = j.slot(2), j.slot(4)
                wait(e, s_zr, j.at(1))
                wait(e, l_in[k], 32 * j.uses(4))
                if not j.first(2):
                    wait(e, s_d2, j.at(-1))
                for s in range(4):
                    mm = e.matmul(Z[q][:, s * 128:(s + 1) * 128], ZR[:, k, s * 128:(s + 1) * 128], WB[:, k, :],
                                  start=True, stop=True)
                mm.then_inc(s_p1, 1)

            def p2(j):
                q, k = j.slot(2), j.slot(4)
                wait(e, s_a1, j.at(1))
                if not j.first(2):
                    wait(e, s_d3, j.at(-1))
                for s in range(4):
                    mm = e.transpose(ET[q][:, s * 128:(s + 1) * 128], EE[:, q, 0, s * 128:(s + 1) * 128], ident[:, :])
                mm.then_inc(s_p2t, 1)
                if not j.first(1):
                    wait(e, s_d4a, j.at())
                for a in range(3):
                    for s in range(4):
                        lhs = EE[:, q, a, s * 128:(s + 1) * 128] if a < 2 else onesb[:, :]
                        rhs = oh[:, k, s, :] if a < 2 else ohb[:, q, s, :]
                        mm = e.matmul(S1[:, a * W:(a + 1) * W], lhs, rhs, start=(s == 0), stop=(s == 3))
                mm.then_inc(s_p2, 1)

            def p3(j):
                q = j.slot(2)
                wait(e, s_d3, j.at(1))
                if not j.first(1):
                    wait(e, s_a2, j.at())
                for a in range(2):
                    for s in range(4):
                        mm = e.transpose(BK[a][:, s * 128:(s + 1) * 128], ST[:, q, a, s * 128:(s + 1) * 128], ident[:, :])
                mm.then_inc(s_p3, 1)

            def p4(j):
                q, k = j.slot(2), j.slot(4)
                wait(e, s_a2, j.at(1))
                wait(e, s_ohl, j.at(1))
                if not j.first(1):
                    wait(e, s_d4b, j.at())
                for a in range(2):
                    for s in range(4):
                        mm = e.matmul(S2[:, a * W:(a + 1) * W], BS[:, q, a, s * 128:(s + 1) * 128], ohl[:, k, s, :],
                                      start=(s == 0), stop=(s == 3))
                mm.then_inc(s_p4, 1)

            pipeline(e, T, U, D, [(5, p3), (1, p1), (6, p4), (3, p2)])


def steps(n, stages):
    for i in range(n + max(lag for lag, _ in stages)):
        for lag, f in stages:
            if 0 <= i - lag < n:
                f(i - lag)


def recycle(nc, used):
    with nc.Block() as blk:
        @blk.gpsimd
        def _(e):
            for s in used:
                e.sem_clear(s)
    for s in used:
        nc.release_semaphore(s)


def phase_n1(nc, d, v):
    sbt, pst = v["sbt"], v["pst"]
    used = []

    def sem(name):
        used.append(nc.alloc_semaphore(name=name))
        return used[-1]

    acc, ident, ones, dinv = v["acc"], v["ident"], v["ones"], v["dinv"]
    X1D, XS, DQ = v["X1D"], v["XS"], v["DQ"]
    NG = len(GROUPS)
    with ExitStack() as ph:
        w1 = sbt(ph, "w1", [128, 13, 128])
        w2 = sbt(ph, "w2", [128, 128])
        b1 = sbt(ph, "b1", [128, 1])
        b2 = sbt(ph, "b2", [128, 1])
        xt = sbt(ph, "xt", [128, 3, 512])
        mean = sbt(ph, "mean", [128, 2, 512])
        std = sbt(ph, "std", [128, 2, 512])
        dq = sbt(ph, "dq", [128, 3, 3, 512])
        nm = sbt(ph, "nm", [128, 3, NB])
        nt = sbt(ph, "nt", [128, 4, NB])
        rt = sbt(ph, "rt", [NB, 3, 128])
        tmp = sbt(ph, "tmp1", [128, 4, 512])
        hh = sbt(ph, "hh", [128, 2, 512])
        xb = sbt(ph, "xb", [128, 2, 512])
        rr = sbt(ph, "rr", [128, 2, 512])
        x1 = sbt(ph, "x1", [128, 2, 4, 128])
        xs = sbt(ph, "xs", [128, 2, 4, 128])
        bn = sbt(ph, "bn1", [128, 4, 6])
        mv = sbt(ph, "mv1", [128, 2, 4, 2])
        vd = sbt(ph, "vd1", [128, 2, 4])
        PP = [pst(ph, f"PP{k}", [128, 512]) for k in range(3)]
        PY = pst(ph, "PY", [128, 512])
        TR = [pst(ph, f"TR{k}", [128, 512]) for k in range(2)]
        XT = pst(ph, "XT", [128, 512])
        DG = pst(ph, "DG", [128, 512])
        n_w = sem("n_w")
        n_x = [sem(f"n_x{k}") for k in range(3)]
        n_dq = sem("n_dq")
        n_q = [sem(f"n_q{k}") for k in range(3)]
        s_dg = sem("n_dg")
        s_d1 = sem("n_d1")
        s_lg = sem("n_lg")
        s_nm = sem("n_nm")
        s_tq = sem("n_tq")
        s_rt = sem("n_rt")
        n_o = [sem(f"n_o{k}") for k in range(2)]
        s_var = sem("n_var")
        s_sq = sem("n_sq")
        s_a2 = sem("n_a2")
        s_b = sem("n_b")
        s_d = sem("n_d")
        s_h = sem("n_h")
        s_y = sem("n_y")
        s_e = sem("n_e")
        s_r = sem("n_r")
        s_f1 = sem("n_f1")
        s_rs = sem("n_rs")
        s_f2 = sem("n_f2")
        s_s = sem("n_s")
        s_k = sem("n_k")
        s_v = sem("n_v")
        blk = ph.enter_context(nc.Block())

        def cols(g):
            o, n = GROUPS[g]
            return slice(o, o + n), n, n // 128

        @blk.sync
        def _(e):
            e.dma_start(w1[:, :, :], d["w1"].rearrange("(k p) f -> p k f", p=128)).then_inc(n_w, 16)
            e.dma_start(w2[:, :], d["w2"]).then_inc(n_w, 16)
            e.dma_start(b1[:, :], d["b1"]).then_inc(n_w, 16)
            e.dma_start(b2[:, :], d["b2"]).then_inc(n_w, 16)

            def load(g):
                c, n, _ = cols(g)
                if g >= 3:
                    e.wait_ge(s_h, g - 2)
                e.dma_start(xt[:, g % 3, 0:n], d["xT"][:, c]).then_inc(n_x[g % 3], 16)
                if g >= 3:
                    e.wait_ge(s_d, g - 2)
                if g == 0:
                    e.wait_ge(s_rt, 1)
                    e.dma_start(DQ.rearrange("q (b n) -> b q n", n=128), rt[:, :, :]).then_inc(n_dq, 16)
                    e.wait_ge(n_dq, 16)
                e.dma_start(dq[:, g % 3, :, 0:n], DQ[:, c].partition_broadcast(128)).then_inc(n_q[g % 3], 16)

            def store(g):
                c, n, nb = cols(g)
                e.wait_ge(s_f2, g + 1)
                for t, s in ((X1D, x1), (XS, xs)):
                    e.dma_start(t[c, :].rearrange("(b p) f -> p b f", p=128), s[:, g % 2, 0:nb, :])\
                     .then_inc(n_o[g % 2], 16)

            steps(NG, [(0, load), (5, store)])
            for k in range(2):
                e.wait_ge(n_o[k], 32 * len(range(k, NG, 2)))

        @blk.vector
        def _(e):
            ch = Chain(e, s_v)

            e.wait_ge(s_dg, 1)
            ch(e.tensor_copy(nt[:, 0, :], DG[:, 0:NB]))
            ch.sync()
            ch(e.tensor_scalar(nt[:, 1, :], nt[:, 0, :], 1.0, None, ALU.max))
            ch(e.tensor_scalar(nt[:, 2, :], nt[:, 0, :], 1.0, None, ALU.add))
            ch.raises(s_d1)
            ch(e.reciprocal(nm[:, 0, :], nt[:, 1, :]))
            e.wait_ge(s_lg, 1)
            ch(e.reciprocal(dinv[:, :], nt[:, 2, :]))
            ch(e.tensor_scalar(nm[:, 1, :], nt[:, 3, :], 1.0 / 2.5, None, ALU.mult))
            ch.sync()
            ch(e.tensor_scalar(nt[:, 1, :], nt[:, 3, :], EPS, 1.0 / 2.5, ALU.max, ALU.mult))
            ch.sync()
            ch(e.reciprocal(nt[:, 2, :], nt[:, 1, :]))
            ch.sync()
            ch(e.scalar_tensor_tensor(nm[:, 2, :], nt[:, 0, :], 1.0, nt[:, 2, :], ALU.min, ALU.mult))
            ch.raises(s_nm)

            def a(g):
                c, n, _ = cols(g)
                q = g % 2
                t = lambda k: tmp[:, k, 0:n]
                r = dq[:, g % 3, 0, 0:n]
                ch.sync()
                e.wait_ge(n_q[g % 3], 16 * (g // 3 + 1))
                if g >= 2:
                    e.wait_ge(s_b, g - 1)
                ch(e.tensor_tensor(mean[:, q, 0:n], acc[:, 0, c], r, ALU.mult))
                ch(e.tensor_tensor(t(0), acc[:, 1, c], r, ALU.mult))
                ch.sync()
                ch(e.tensor_tensor(t(1), mean[:, q, 0:n], mean[:, q, 0:n], ALU.mult))
                ch.sync()
                ch(e.tensor_tensor(t(0), t(0), t(1), ALU.subtract))
                ch.sync()
                ch(e.tensor_scalar(std[:, q, 0:n], t(0), 0.0, EPS, ALU.max, ALU.add))
                ch.raises(s_var)

            def a2(g):
                c, n, _ = cols(g)
                q = g % 2
                e.wait_ge(s_sq, g + 1)
                ch(e.scalar_tensor_tensor(std[:, q, 0:n], acc[:, 2, c], 1.0, std[:, q, 0:n], ALU.min, ALU.mult))
                ch.raises(s_a2)

            def dd(g):
                _, n, _ = cols(g)
                q = g % 2
                e.wait_ge(s_b, g + 1)
                ch(e.tensor_tensor(tmp[:, 2, 0:n], PP[1][:, 0:n], dq[:, g % 3, 1, 0:n], ALU.mult))
                ch(e.tensor_tensor(tmp[:, 3, 0:n], PP[2][:, 0:n], dq[:, g % 3, 2, 0:n], ALU.mult))
                ch.sync()
                ch(e.tensor_tensor(tmp[:, 2, 0:n], tmp[:, 2, 0:n], tmp[:, 3, 0:n], ALU.add))
                ch.sync()
                if g >= 2:
                    e.wait_ge(s_y, g - 1)
                ch(e.tensor_tensor(hh[:, q, 0:n], PP[0][:, 0:n], tmp[:, 2, 0:n], ALU.add))
                ch.raises(s_d)

            def ee(g):
                _, n, _ = cols(g)
                e.wait_ge(s_y, g + 1)
                e.wait_ge(s_h, g + 1)
                if g >= 2:
                    e.wait_ge(s_r, g - 1)
                ch(e.tensor_tensor(rr[:, g % 2, 0:n], PY[:, 0:n], xb[:, g % 2, 0:n], ALU.add))
                ch.raises(s_e)

            def f1(g):
                _, n, nb = cols(g)
                q = g % 2
                e.wait_ge(s_r, g + 1)
                for b in range(nb):
                    ch(e.bn_stats(bn[:, b, :], TR[q][:, b * 128:(b + 1) * 128]))
                ch.sync()
                for b in range(nb):
                    ch(e.bn_aggr(mv[:, q, b, :], bn[:, b, :]))
                ch.sync()
                ch(e.tensor_scalar(vd[:, q, 0:nb], mv[:, q, 0:nb, 1], EPS, None, ALU.add))
                ch.raises(s_f1)

            def f2(g):
                c, n, nb = cols(g)
                q = g % 2
                e.wait_ge(s_rs, g + 1)
                ch(e.reciprocal(vd[:, q, 0:nb], vd[:, q, 0:nb]))
                ch.sync()
                if g >= 2:
                    e.wait_ge(n_o[q], 32 * (g // 2))
                    e.wait_ge(s_s, g - 1)
                for b in range(nb):
                    ch(e.tensor_scalar(x1[:, q, b, :], TR[q][:, b * 128:(b + 1) * 128], mv[:, q, b, 0:1],
                                       vd[:, q, b:b + 1], ALU.subtract, ALU.mult))
                ch.sync()
                for b in range(nb):
                    o = c.start // 128 + b
                    ch(e.tensor_scalar(xs[:, q, b, :], x1[:, q, b, :], dinv[:, o:o + 1], None, ALU.mult))
                ch.raises(s_f2)

            steps(NG, [(2, dd), (1, a2), (3, ee), (4, f1), (5, f2), (0, a)])

        @blk.scalar
        def _(e):
            e.wait_ge(n_w, 64)

            e.wait_ge(s_d1, 1)
            e.activation(nt[:, 3, :], nt[:, 2, :], ACT.Ln)
            e.activation(nt[:, 2, :], nt[:, 2, :], ACT.Sqrt).then_inc(s_lg, 1)
            e.wait_ge(s_tq, 1)
            e.copy(rt[:, :, :], XT[0:NB, 0:384].rearrange("p (q n) -> p q n", q=3)).then_inc(s_rt, 1)

            def roots(g):
                c, n, _ = cols(g)
                q = g % 2
                e.wait_ge(s_var, g + 1)
                e.activation(std[:, q, 0:n], std[:, q, 0:n], ACT.Sqrt).then_inc(s_sq, 1)

            def h(g):
                _, n, _ = cols(g)
                q = g % 2
                e.wait_ge(s_d, g + 1)
                e.activation(hh[:, q, 0:n], hh[:, q, 0:n], ACT.Relu, bias=b1[:, 0:1])
                e.wait_ge(n_x[g % 3], 16 * (g // 3 + 1))
                if g >= 2:
                    e.wait_ge(s_e, g - 1)
                e.activation(xb[:, q, 0:n], xt[:, g % 3, 0:n], ACT.Identity, bias=b2[:, 0:1], scale=2.0).then_inc(s_h, 1)

            def rs(g):
                nb = cols(g)[2]
                e.wait_ge(s_f1, g + 1)
                e.activation(vd[:, g % 2, 0:nb], vd[:, g % 2, 0:nb], ACT.Sqrt).then_inc(s_rs, 1)

            def k(g):
                c, n, _ = cols(g)
                e.wait_ge(s_s, g + 1)
                e.copy(acc[:, 0, c], XT[:, 0:n]).then_inc(s_k, 1)

            steps(NG, [(2, h), (4, rs), (6, k), (0, roots)])

        @blk.tensor
        def _(e):
            for b in range(NB):
                mm = e.matmul(DG[:, b:b + 1], acc[0:1, 2, b * 128:(b + 1) * 128], ones[0:1, 0:1], start=True, stop=True)
            mm.then_inc(s_dg, 1)
            e.wait_ge(s_nm, 1)
            for k in range(3):
                mm = e.transpose(XT[0:NB, k * 128:(k + 1) * 128], nm[:, k, :], ident[:, :])
            mm.then_inc(s_tq, 1)
            e.wait_ge(n_w, 64)

            def y(g):
                _, n, _ = cols(g)
                e.wait_ge(s_h, g + 1)
                if g >= 1:
                    e.wait_ge(s_e, g)
                e.matmul(PY[:, 0:n], w2[:, :], hh[:, g % 2, 0:n], start=True, stop=True).then_inc(s_y, 1)

            def r(g):
                c, n, nb = cols(g)
                q = g % 2
                e.wait_ge(s_e, g + 1)
                if g >= 2:
                    e.wait_ge(s_f2, g - 1)
                for b in range(nb):
                    mm = e.transpose(TR[q][:, b * 128:(b + 1) * 128], rr[:, q, b * 128:(b + 1) * 128], ident[:, :])
                mm.then_inc(s_r, 1)

            def s(g):
                _, n, nb = cols(g)
                e.wait_ge(s_f2, g + 1)
                if g >= 1:
                    e.wait_ge(s_k, g)
                for b in range(nb):
                    mm = e.transpose(XT[:, b * 128:(b + 1) * 128], xs[:, g % 2, b, :], ident[:, :])
                mm.then_inc(s_s, 1)

            def b(g):
                c, n, _ = cols(g)
                q = g % 2
                e.wait_ge(n_x[g % 3], 16 * (g // 3 + 1))
                e.wait_ge(s_a2, g + 1)
                if g >= 1:
                    e.wait_ge(s_d, g)
                agg = (mean[:, q, 0:n], acc[:, 3, c], acc[:, 4, c], std[:, q, 0:n])
                e.matmul(PP[0][:, 0:n], w1[:, 0, :], xt[:, g % 3, 0:n], start=True, stop=False)
                for p in range(3):
                    for k in range(4):
                        mm = e.matmul(PP[p][:, 0:n], w1[:, 1 + 4 * p + k, :], agg[k],
                                      start=(p > 0 and k == 0), stop=(k == 3))
                mm.then_inc(s_b, 1)

            steps(NG, [(3, y), (4, r), (6, s), (1, b)])
    recycle(nc, used)


def phase_gcn(nc, d, v):
    sem, sbt, pst = v["sem"], v["sbt"], v["pst"]
    acc, baseF, tb, iotaW, XS = v["acc"], v["baseF"], v["tb"], v["iotaW"], v["XS"]
    with ExitStack() as ph:
        meta = sbt(ph, "metac", [128, 4, 12], I32)
        G = sbt(ph, "Gc", [128, 4, 4, 128])
        oh = sbt(ph, "ohc", [128, 2, 4, W])
        iob = sbt(ph, "iobc", [128, 2, W])
        S = [pst(ph, f"Sc{k}", [128, 512]) for k in range(2)]
        l_mt = [sem(f"c_mt{k}") for k in range(4)]
        l_g = [sem(f"c_g{k}") for k in range(4)]
        s_iob = sem("c_iob")
        s_oh = sem("c_oh")
        s_mm = sem("c_mm")
        s_acc = sem("c_acc")
        s_pool = v["s_pool"]
        s_sync = v["s_sync"]
        blk = ph.enter_context(nc.Block())
        U, D = 4, 4

        @blk.sync
        def _(e):
            T = load_T(e, tb, 0)

            def load(j):
                k = j.slot(4)
                c = chunk_of(e, tb, j)
                before = 64 * j.uses(4, -1), j.at(-3)
                if not j.first(4):
                    wait_sync(e, l_g[k], before[0], s_sync)
                    wait_sync(e, s_oh, before[1], s_sync)
                e.dma_start(meta[:, k, :], d["meta"][ds(c, 1), :, :].rearrange("a p s -> (a p) s")).then_inc(l_mt[k], 16)

            pipeline(e, T, U, D, [(0, load)])

        @blk.gpsimd
        def _(e):
            T = load_T(e, tb, 0)

            def gather(j):
                k = j.slot(4)
                wait(e, l_mt[k], 16 * j.uses(4))
                if not j.first(4):
                    wait(e, s_mm, j.at(-3))
                e.sem_inc(s_pool, 1)
                for s in range(4):
                    e.indirect_dma_start(G[:, k, s, :], None, XS,
                                         bass.IndirectOffsetOnAxis(ap=meta[:, k, s:s + 1], axis=0)).then_inc(l_g[k], 16)

            pipeline(e, T, U, D, [(0, gather)])

        @blk.vector
        def _(e):
            T = load_T(e, tb, 0)

            def onehot(j):
                k, q = j.slot(4), j.slot(2)
                e.tensor_scalar(iob[:, q, :], iotaW[:, :], baseF[:, ds(j.at(), 1)], None, ALU.add).then_inc(s_iob, 1)
                wait(e, l_mt[k], 16 * j.uses(4))
                if not j.first(2):
                    wait(e, s_mm, j.at(-1))
                wait(e, s_iob, j.at(1))
                e.tensor_tensor(oh[:, q, :, :], iob[:, q:q + 1, :].to_broadcast([128, 4, W]),
                                meta[:, k, 4:8].unsqueeze(2).to_broadcast([128, 4, W]),
                                ALU.is_equal).then_inc(s_oh, 1)

            def add(j):
                b = base_of(e, tb, j)
                wait(e, s_mm, j.at(1))
                if not j.first(1):
                    wait(e, s_acc, j.at())
                a = acc[:, 0, ds(b, W)]
                e.tensor_tensor(a, a, S[j.slot(2)][:, 0:W], ALU.add).then_inc(s_acc, 1)

            pipeline(e, T, U, D, [(0, onehot), (1, add)])

        @blk.tensor
        def _(e):
            T = load_T(e, tb, 0)

            def mm(j):
                k, q = j.slot(4), j.slot(2)
                wait(e, s_oh, j.at(1))
                wait(e, l_g[k], 64 * j.uses(4))
                if not j.first(2):
                    wait(e, s_acc, j.at(-1))
                for s in range(4):
                    m = e.matmul(S[q][:, 0:W], G[:, k, s, :], oh[:, q, s, :], start=(s == 0), stop=(s == 3))
                m.then_inc(s_mm, 1)

            pipeline(e, T, U, D, [(0, mm)])


def phase_n2(nc, d, v):
    sem, sbt, pst = v["sem"], v["sbt"], v["pst"]
    acc, ident, ones, dinv = v["acc"], v["ident"], v["ones"], v["dinv"]
    TAB, ADT = v["TAB"], v["ADT"]
    NG = len(GROUPS)
    with ExitStack() as ph:
        gw = sbt(ph, "gw", [128, 128])
        gwT = sbt(ph, "gwT", [128, 2, 128])
        at = sbt(ph, "at", [128, 2, 2])
        gb = sbt(ph, "gb", [128, 3, 128])
        vv = sbt(ph, "vv", [128, 3, 2])
        tt = sbt(ph, "tt", [128, 2, 4, 128])
        zz = sbt(ph, "zz", [128, 2, 4, 128])
        ts = sbt(ph, "ts", [128, 2, 4, 130])
        adt = sbt(ph, "adt", [128, 2, 4, 2])
        bn = sbt(ph, "bn2", [128, 4, 6])
        mv = sbt(ph, "mv2", [128, 2, 4, 2])
        rs = sbt(ph, "rs2", [128, 2, 4])
        lr = sbt(ph, "lr", [1, 2, 512])
        Q = [pst(ph, f"Q{k}", [128, 512]) for k in range(2)]
        HT = pst(ph, "HT", [128, 512])
        AB = pst(ph, "AB", [128, 512])
        LR = [pst(ph, f"LR{k}", [128, 512]) for k in range(2)]
        PV = pst(ph, "PV", [128, 512])
        w = sem("m_w")
        s_o = [sem(f"m_o{k}") for k in range(2)]
        s_pv = sem("m_pv")
        s_vv = sem("m_vv")
        s_q = sem("m_q")
        s_f1 = sem("m_f1")
        s_rs = sem("m_rs")
        s_f2 = sem("m_f2")
        s_h = sem("m_h")
        s_t = sem("m_t")
        s_c1 = sem("m_c1")
        s_c2 = sem("m_c2")
        s_ab = sem("m_ab")
        s_g = sem("m_g")
        s_v = sem("m_v")
        blk = ph.enter_context(nc.Block())

        def cols(g):
            o, n = GROUPS[g]
            return slice(o, o + n), n, n // 128

        @blk.sync
        def _(e):
            e.dma_start(gw[:, :], d["gcnw"]).then_inc(w, 16)
            e.dma_start(gwT[:, :, :], d["gatwT"].rearrange("(h c) f -> c h f", h=2)).then_inc(w, 16)
            e.dma_start(at[:, 0, :], d["atts"]).then_inc(w, 16)
            e.dma_start(at[:, 1, :], d["attd"]).then_inc(w, 16)
            for k, t in enumerate(("gcnb", "gamma", "beta")):
                e.dma_start(gb[:, k, :], d[t].partition_broadcast(128)).then_inc(w, 16)

            def store(g):
                c, n, nb = cols(g)
                q = g % 2
                e.wait_ge(s_g, g + 1)
                e.dma_start(TAB[c, :].rearrange("(b p) f -> p b f", p=128), ts[:, q, 0:nb, :]).then_inc(s_o[q], 16)
                e.dma_start(ADT[c, :].rearrange("(b p) f -> p b f", p=128), adt[:, q, 0:nb, :]).then_inc(s_o[q], 16)

            steps(NG, [(0, store)])
            for k in range(2):
                e.wait_ge(s_o[k], 32 * len(range(k, NG, 2)))

        @blk.tensor
        def _(e):
            e.wait_ge(w, 112)
            for h in range(2):
                for k in range(2):
                    mm = e.matmul(PV[:, 2 * k + h:2 * k + h + 1], gwT[:, h, :], at[:, k, h:h + 1], start=True, stop=True)
            mm.then_inc(s_pv, 1)

            def q(g):
                c, n, nb = cols(g)
                if g >= 2:
                    e.wait_ge(s_f1, g - 1)
                for b in range(nb):
                    mm = e.matmul(Q[g % 2][:, b * 128:(b + 1) * 128], acc[:, 0, c.start + b * 128:c.start + (b + 1) * 128],
                                  gw[:, :], start=True, stop=True)
                mm.then_inc(s_q, 1)

            def t(g):
                c, n, nb = cols(g)
                e.wait_ge(s_h, g + 1)
                if g >= 1:
                    e.wait_ge(s_c1, g)
                    e.wait_ge(s_c2, g)
                for b in range(nb):
                    mm = e.transpose(HT[:, b * 128:(b + 1) * 128], ts[:, g % 2, b, 0:128], ident[:, :])
                mm.then_inc(s_t, 1)

            def a(g):
                c, n, nb = cols(g)
                e.wait_ge(s_c1, g + 1)
                e.wait_ge(s_vv, 1)
                if g >= 1:
                    e.wait_ge(s_g, g)
                for b in range(nb):
                    e.matmul(AB[:, b * 4:b * 4 + 4], acc[:, 1, c.start + b * 128:c.start + (b + 1) * 128],
                             vv[:, 0:2, :].rearrange("p k h -> p (k h)"), start=True, stop=True)
                for h in range(2):
                    mm = e.matmul(LR[h][0:1, 0:n], vv[:, 2, h:h + 1], acc[:, 1, c], start=True, stop=True)
                mm.then_inc(s_ab, 1)

            steps(NG, [(2, t), (3, a), (0, q)])

        @blk.vector
        def _(e):
            ch = Chain(e, s_v)
            e.wait_ge(w, 112)
            ch(e.memset(acc[32:33, 3:5, :], 1.0))
            e.wait_ge(s_pv, 1)
            ch(e.tensor_copy(vv[:, 0:2, :].rearrange("p k h -> p (k h)"), PV[:, 0:4]))
            ch.sync()
            ch(e.tensor_tensor(vv[:, 2, :], vv[:, 0, :], vv[:, 1, :], ALU.add))
            ch.raises(s_vv)

            def f1(g):
                c, n, nb = cols(g)
                q = g % 2
                e.wait_ge(s_q, g + 1)
                for b in range(nb):
                    o = c.start // 128 + b
                    ch(e.scalar_tensor_tensor(tt[:, q, b, :], Q[q][:, b * 128:(b + 1) * 128], dinv[:, o:o + 1],
                                              gb[:, 0, :], ALU.mult, ALU.add))
                ch.sync()
                for b in range(nb):
                    ch(e.bn_stats(bn[:, b, :], tt[:, q, b, :]))
                ch.sync()
                for b in range(nb):
                    ch(e.bn_aggr(mv[:, q, b, :], bn[:, b, :]))
                ch.sync()
                ch(e.tensor_scalar(rs[:, q, 0:nb], mv[:, q, 0:nb, 1], EPS, None, ALU.add))
                ch.raises(s_f1)

            def f2(g):
                c, n, nb = cols(g)
                q = g % 2
                e.wait_ge(s_rs, g + 1)
                ch(e.reciprocal(rs[:, q, 0:nb], rs[:, q, 0:nb]))
                ch.sync()
                for b in range(nb):
                    ch(e.tensor_scalar(tt[:, q, b, :], tt[:, q, b, :], mv[:, q, b, 0:1], rs[:, q, b:b + 1],
                                       ALU.subtract, ALU.mult))
                ch.sync()
                bc = lambda k: gb[:, k:k + 1, :].to_broadcast([128, nb, 128])
                ch(e.tensor_tensor(tt[:, q, 0:nb, :], tt[:, q, 0:nb, :], bc(1), ALU.mult))
                ch.sync()
                if g >= 2:
                    e.wait_ge(s_h, g - 1)
                ch(e.tensor_tensor(zz[:, q, 0:nb, :], tt[:, q, 0:nb, :], bc(2), ALU.add))
                ch.raises(s_f2)

            def c1(g):
                c, n, nb = cols(g)
                e.wait_ge(s_t, g + 1)
                ch(e.tensor_copy(acc[:, 1, c], HT[:, 0:n]))
                ch.raises(s_c1)

            def gg(g):
                c, n, nb = cols(g)
                q = g % 2
                e.wait_ge(s_ab, g + 1)
                AV = AB[:, 0:4 * nb].rearrange("p (b k) -> p b k", k=4)
                if g >= 2:
                    e.wait_ge(s_o[q], 32 * (g // 2))
                ch(e.tensor_copy(ts[:, q, 0:nb, 128:130], AV[:, :, 0:2]))
                ch(e.tensor_copy(adt[:, q, 0:nb, :], AV[:, :, 2:4]))
                for h in range(2):
                    ch(e.tensor_scalar(lr[0:1, h, 0:n], LR[h][0:1, 0:n], 0.2, None, ALU.mult))
                ch.sync()
                for h in range(2):
                    ch(e.tensor_tensor(acc[0:1, 3 + h, c], lr[0:1, h, 0:n], LR[h][0:1, 0:n], ALU.max))
                ch.raises(s_g)

            steps(NG, [(2, c1), (3, gg), (1, f2), (0, f1)])

        @blk.scalar
        def _(e):
            def r(g):
                nb = cols(g)[2]
                e.wait_ge(s_f1, g + 1)
                e.activation(rs[:, g % 2, 0:nb], rs[:, g % 2, 0:nb], ACT.Sqrt).then_inc(s_rs, 1)

            def h(g):
                nb, q = cols(g)[2], g % 2
                e.wait_ge(s_f2, g + 1)
                if g >= 2:
                    e.wait_ge(s_o[q], 32 * (g // 2))
                    e.wait_ge(s_t, g - 1)
                e.activation(ts[:, q, 0:nb, 0:128], zz[:, q, 0:nb, :], ACT.Silu).then_inc(s_h, 1)

            def c2(g):
                c, n, nb = cols(g)
                e.wait_ge(s_t, g + 1)
                e.wait_ge(s_c1, g + 1)
                e.copy(acc[:, 2, c], HT[:, 0:n]).then_inc(s_c2, 1)

            steps(NG, [(2, c2), (1, h), (0, r)])


def phase_gat(nc, d, v):
    sem, sbt, pst = v["sem"], v["sbt"], v["pst"]
    acc, baseF, tb, iotaW = v["acc"], v["baseF"], v["tb"], v["iotaW"]
    ident, ones, TAB, ADT = v["ident"], v["ones"], v["TAB"], v["ADT"]
    with ExitStack() as ph:
        meta = sbt(ph, "metat", [128, 8, 12], I32)
        G = sbt(ph, "Gt", [128, 8, 4, 130])
        ad = sbt(ph, "ad", [128, 8, 1])
        iob = sbt(ph, "iobt", [128, 2, W])
        neq = sbt(ph, "neqt", [128, 2, 4, W])
        M = sbt(ph, "M", [128, 2, 4, 2, W])
        TE = sbt(ph, "TE", [128, 2, CH])
        EX = sbt(ph, "EX", [128, 2, CH])
        P = sbt(ph, "P", [128, 2, CH])
        lt = sbt(ph, "lt", [128, 2, 3])
        ln = sbt(ph, "ln", [1, 2, 2, W])
        df = sbt(ph, "df", [1, 2, 2, W])
        sc = sbt(ph, "sc", [1, 4, 2 * W])
        nl = sbt(ph, "nl", [128, 2, 1])
        dsum = sbt(ph, "dsum", [128, 4, 1])
        neg = sbt(ph, "neg", [1, 1])
        MT = [pst(ph, f"MT{k}", [128, CH]) for k in range(2)]
        LT = pst(ph, "LT", [128, 512])
        NL = pst(ph, "NL", [128, 512])
        PT = [pst(ph, f"PT{k}", [128, CH]) for k in range(2)]
        SR = [pst(ph, f"SR{k}", [128, 512]) for k in range(2)]
        l_mt = [sem(f"g_mt{k}") for k in range(8)]
        l_g = [sem(f"g_g{k}") for k in range(8)]
        s_iob = sem("g_iob")
        s_nq = sem("g_nq")
        s_m = sem("g_m")
        s_t1 = sem("g_t1")
        s_mx = sem("g_mx")
        s_lt0 = sem("g_lt0")
        s_lt = sem("g_lt")
        s_a1 = sem("g_a1")
        s_t2 = sem("g_t2")
        s_ln = sem("g_ln")
        s_df = sem("g_df")
        s_st = sem("g_st")
        s_lk = sem("g_lk")
        s_sc = sem("g_sc")
        s_t3 = sem("g_t3")
        s_nl = sem("g_nl")
        s_ex = sem("g_ex")
        s_t4 = sem("g_t4")
        s_p = sem("g_p")
        s_t5 = sem("g_t5")
        s_u1 = sem("g_u1")
        s_u = sem("g_u")
        s_i = sem("g_i")
        s_pool = v["s_pool"]
        s_sync = v["s_sync"]
        blk = ph.enter_context(nc.Block())
        U, D = 8, 8

        @blk.sync
        def _(e):
            T = load_T(e, tb, 1)

            def load(j):
                k = j.slot(8)
                c, b = chunk_of(e, tb, j), base_of(e, tb, j)
                before = 64 * j.uses(8, -1), j.at(-7)
                if not j.first(8):
                    wait_sync(e, l_g[k], before[0], s_sync)
                    for s in (s_nq, s_a1, s_lt0):
                        wait_sync(e, s, before[1], s_sync)
                e.dma_start(meta[:, k, :], d["meta"][ds(c, 1), :, :].rearrange("a p s -> (a p) s")).then_inc(l_mt[k], 16)
                for h in range(2):
                    e.dma_start(ad[h * W:(h + 1) * W, k, :], ADT[ds(b, W), h:h + 1],
                                allow_slow_non_contiguous=True).then_inc(l_mt[k], 16)

            pipeline(e, T, U, D, [(0, load)])

        @blk.gpsimd
        def _(e):
            T = load_T(e, tb, 1)

            def gather(j):
                k = j.slot(8)
                wait(e, l_mt[k], 48 * j.uses(8))
                if not j.first(8):
                    wait(e, s_t5, j.at(-7))
                e.sem_inc(s_pool, 1)
                for s in range(4):
                    e.indirect_dma_start(G[:, k, s, :], None, TAB,
                                         bass.IndirectOffsetOnAxis(ap=meta[:, k, s:s + 1], axis=0)).then_inc(l_g[k], 16)

            pipeline(e, T, U, D, [(0, gather)])

        @blk.vector
        def _(e):
            e.memset(neg[:, :], -1.0).then_inc(s_i, 1)
            T = load_T(e, tb, 1)
            base = {}
            regs = [e.alloc_register(f"g_base{k}") for k in range(8)]
            L = lambda b: acc[0:1, 3:5, ds(b, W)]
            UD = lambda b: ((slice(0, 128), acc[:, 1:3, ds(b, W)], 0), (slice(32, 33), acc[32:33, 3:5, ds(b, W)], 4 * W))
            sr = lambda j, p, o: SR[j.slot(2)][p, o:o + 2 * W].rearrange("p (h n) -> p h n", h=2)

            def window(j):
                q = j.slot(2)
                if not j.first(2):
                    wait(e, s_nq, j.at(-1))
                e.tensor_scalar(iob[:, q, :], iotaW[:, :], baseF[:, ds(j.at(), 1)], None, ALU.add).then_inc(s_iob, 1)

            def outside(j):
                k, q = j.slot(8), j.slot(2)
                wait(e, l_mt[k], 48 * j.uses(8))
                wait(e, s_iob, j.at(1))
                if not j.first(2):
                    wait(e, s_m, j.at(-1))
                e.tensor_tensor(neq[:, q, :, :], iob[:, q:q + 1, :].to_broadcast([128, 4, W]),
                                meta[:, k, 4:8].unsqueeze(2).to_broadcast([128, 4, W]),
                                ALU.not_equal).then_inc(s_nq, 1)

            def masked(j):
                k, q = j.slot(8), j.slot(2)
                wait(e, l_g[k], 64 * j.uses(8))
                wait(e, s_nq, j.at(1))
                if not j.first(2):
                    wait(e, s_t1, j.at(-1))
                for h in range(2):
                    i = e.scalar_tensor_tensor(M[:, q, :, h, :], neq[:, q, :, :], -BIG,
                                               G[:, k, :, 128 + h:129 + h].to_broadcast([128, 4, W]),
                                               ALU.mult, ALU.add)
                i.then_inc(s_m, 1)

            def highest(j):
                q = j.slot(2)
                wait(e, s_t1, j.at(1))
                e.tensor_reduce(lt[:, q, 0:1], MT[q][:, :], mybir.AxisListType.X, ALU.max).then_inc(s_mx, 1)

            def score(j):
                k, q = j.slot(8), j.slot(2)
                wait(e, l_mt[k], 48 * j.uses(8))
                wait(e, s_mx, j.at(1))
                e.tensor_tensor(lt[:, q, 1:2], lt[:, q, 0:1], ad[:, k, :], ALU.add).then_inc(s_lt0, 1)

            def leak_score(j):
                q = j.slot(2)
                if not j.first(2):
                    wait(e, s_t2, j.at(-1))
                wait(e, s_lt0, j.at(1))
                e.scalar_tensor_tensor(lt[:, q, 2:3], lt[:, q, 1:2], 0.2, lt[:, q, 1:2], ALU.mult, ALU.max).then_inc(s_lt, 1)

            def new_max(j):
                q = j.slot(2)
                base[0] = keep(e, regs, j, base_of(e, tb, j))
                wait(e, s_t2, j.at(1))
                if not j.first(2):
                    wait(e, s_t3, j.at(-1))
                    wait(e, s_st, j.at(-1))
                if not j.first(1):
                    wait(e, s_st, j.at())
                e.tensor_tensor(ln[:, q, :, :], L(base[0]), LT[0:1, 0:2 * W].rearrange("p (h n) -> p h n", h=2), ALU.max)\
                 .then_inc(s_ln, 1)

            def step_max(j):
                q = j.slot(2)
                if not j.first(2):
                    wait(e, s_sc, j.at(-1))
                wait(e, s_ln, j.at(1))
                e.tensor_tensor(df[:, q, :, :], L(base[0]), ln[:, q, :, :], ALU.subtract).then_inc(s_df, 1)

            def leak(j):
                q = j.slot(2)
                wait(e, s_a1, j.at(1))
                e.scalar_tensor_tensor(TE[:, q, :], TE[:, q, :], 0.2, TE[:, q, :], ALU.mult, ALU.max).then_inc(s_lk, 1)

            def rescale(j):
                base[1] = kept(e, regs, j)
                wait(e, s_t5, j.at(1))
                if not j.first(1):
                    wait(e, s_u, j.at())
                for p, a, o in UD(base[1]):
                    i = e.tensor_tensor(a, a, sr(j, p, 2 * W), ALU.mult)
                i.then_inc(s_u1, 1)

            def add(j):
                wait(e, s_u1, j.at(1))
                for p, a, o in UD(base[1]):
                    i = e.tensor_tensor(a, a, sr(j, p, o), ALU.add)
                i.then_inc(s_u, 1)

            pipeline(e, T, U, D, [(6, rescale), (3, new_max), (1, window), (3, step_max), (6, add),
                                  (2, highest), (1, outside), (2, score), (1, masked), (2, leak_score), (3, leak)])

        @blk.scalar
        def _(e):
            T = load_T(e, tb, 1)

            def a1(j):
                k, q = j.slot(8), j.slot(2)
                wait(e, s_mx, j.at(1))
                wait(e, l_mt[k], 48 * j.uses(8))
                if not j.first(2):
                    wait(e, s_ex, j.at(-1))
                e.activation(TE[:, q, :], MT[q][:, :], ACT.Identity, bias=ad[:, k, 0:1]).then_inc(s_a1, 1)

            def a2(j):
                wait(e, s_df, j.at(1))
                if not j.first(4):
                    wait(e, s_t5, j.at(-3))
                e.activation(sc[:, j.slot(4), :], df[:, j.slot(2), :, :].rearrange("p h n -> p (h n)"), ACT.Exp).then_inc(s_sc, 1)

            def keep_max(j):
                b = base_of(e, tb, j)
                wait(e, s_df, j.at(1))
                e.copy(acc[0:1, 3:5, ds(b, W)], ln[:, j.slot(2), :, :]).then_inc(s_st, 1)

            def a3(j):
                q = j.slot(2)
                wait(e, s_t3, j.at(1))
                e.copy(nl[:, q, :], NL[:, 0:1]).then_inc(s_nl, 1)
                wait(e, s_lk, j.at(1))
                if not j.first(2):
                    wait(e, s_t4, j.at(-1))
                if not j.first(4):
                    wait(e, s_t5, j.at(-3))
                wait(e, s_nl, j.at(1))
                e.activation(EX[:, q, :], TE[:, q, :], ACT.Exp, bias=nl[:, q, 0:1],
                             accum_out=dsum[:, j.slot(4), :]).then_inc(s_ex, 1)

            def a4(j):
                q = j.slot(2)
                wait(e, s_t4, j.at(1))
                if not j.first(2):
                    wait(e, s_t5, j.at(-1))
                e.copy(P[:, q, :], PT[q][:, :]).then_inc(s_p, 1)

            pipeline(e, T, U, D, [(5, a4), (4, a3), (3, a2), (3, keep_max), (2, a1)])

        @blk.tensor
        def _(e):
            e.wait_ge(s_i, 1)
            T = load_T(e, tb, 1)

            def t1(j):
                q = j.slot(2)
                wait(e, s_m, j.at(1))
                if not j.first(2):
                    wait(e, s_a1, j.at(-1))
                for s in range(4):
                    m = e.transpose(MT[q][:, s * 128:(s + 1) * 128],
                                    M[:, q, s, :, :].rearrange("p h n -> p (h n)"), ident[:, :])
                m.then_inc(s_t1, 1)

            def t2(j):
                wait(e, s_lt, j.at(1))
                if not j.first(1):
                    wait(e, s_ln, j.at())
                e.transpose(LT[0:1, 0:2 * W], lt[:, j.slot(2), 2:3], ident[:, :]).then_inc(s_t2, 1)

            def t3(j):
                wait(e, s_ln, j.at(1))
                if not j.first(1):
                    wait(e, s_nl, j.at())
                e.matmul(NL[:, 0:1], ln[:, j.slot(2), :, :].rearrange("p h n -> p (h n)"), neg[:, :],
                         start=True, stop=True).then_inc(s_t3, 1)

            def t4(j):
                q = j.slot(2)
                wait(e, s_ex, j.at(1))
                if not j.first(2):
                    wait(e, s_p, j.at(-1))
                for s in range(4):
                    m = e.transpose(PT[q][:, s * 128:(s + 1) * 128], EX[:, q, s * 128:(s + 1) * 128], ident[:, :])
                m.then_inc(s_t4, 1)

            def t5(j):
                k, q = j.slot(8), j.slot(2)
                wait(e, s_p, j.at(1))
                wait(e, s_sc, j.at(1))
                if not j.first(2):
                    wait(e, s_u, j.at(-1))
                e.matmul(SR[q][:, 2 * W:4 * W], ones[0:1, :], sc[:, j.slot(4), :], start=True, stop=True)
                e.matmul(SR[q][0:64, 4 * W:6 * W], dsum[:, j.slot(4), :].to_broadcast([128, 64]), ident[:, :],
                         start=True, stop=True)
                for s in range(4):
                    m = e.matmul(SR[q][:, 0:2 * W], G[:, k, s, 0:128], P[:, q, s * 128:(s + 1) * 128],
                                 start=(s == 0), stop=(s == 3))
                m.then_inc(s_t5, 1)

            pipeline(e, T, U, D, [(5, t5), (4, t4), (3, t3), (2, t2), (1, t1)])


def phase_n3(nc, d, v, out):
    sem, sbt, pst = v["sem"], v["sbt"], v["pst"]
    acc, ones, X1D = v["acc"], v["ones"], v["X1D"]
    NG = len(GROUPS)
    with ExitStack() as ph:
        gw = sbt(ph, "gw3", [128, 256])
        gb = sbt(ph, "gb3", [128, 3, 128])
        x1 = sbt(ph, "x13", [128, 2, 4, 128])
        tt = sbt(ph, "tt3", [128, 2, 4, 128])
        zz = sbt(ph, "zz3", [128, 2, 4, 128])
        yy = sbt(ph, "yy3", [128, 2, 4, 128])
        oo = sbt(ph, "oo3", [128, 2, 4, 128])
        rd = sbt(ph, "rd", [128, 2, 8])
        bn = sbt(ph, "bn3", [128, 4, 6])
        mv = sbt(ph, "mv3", [128, 2, 2, 4, 2])
        rs = sbt(ph, "rs3", [128, 2, 2, 4])
        H = [[pst(ph, f"H{h}{k}", [128, 512]) for k in range(2)] for h in range(2)]
        DN = pst(ph, "DN", [128, 512])
        w = sem("o_w")
        s_x = [sem(f"o_x{k}") for k in range(2)]
        s_o = [sem(f"o_o{k}") for k in range(2)]
        s_mm = sem("o_mm")
        s_f = [sem("o_f0"), sem("o_f1")]
        s_rs = [sem("o_r0"), sem("o_r1")]
        s_z = sem("o_z")
        s_h = sem("o_h")
        s_y = sem("o_y")
        s_out = sem("o_out")
        s_v = sem("o_v")
        blk = ph.enter_context(nc.Block())

        def cols(g):
            o, n = GROUPS[g]
            return slice(o, o + n), n, n // 128

        @blk.sync
        def _(e):
            e.dma_start(gw[:, :], d["gatw"]).then_inc(w, 16)
            for k, t in enumerate(("gatb", "gamma", "beta")):
                e.dma_start(gb[:, k, :], d[t].partition_broadcast(128)).then_inc(w, 16)

            def load(g):
                c, n, nb = cols(g)
                if g >= 2:
                    e.wait_ge(s_y, g - 1)
                e.dma_start(x1[:, g % 2, 0:nb, :], X1D[c, :].rearrange("(b p) f -> p b f", p=128)).then_inc(s_x[g % 2], 16)

            def store(g):
                c, n, nb = cols(g)
                q = g % 2
                e.wait_ge(s_out, g + 1)
                full = (min(c.stop, N) - c.start) // 128
                if full:
                    e.dma_start(out[c.start:c.start + full * 128, :].rearrange("(b p) f -> p b f", p=128),
                                oo[:, q, 0:full, :]).then_inc(s_o[q], 16)
                else:
                    e.dma_start(out[c.start:N, :], oo[0:N - c.start, q, 0, :]).then_inc(s_o[q], 16)

            steps(NG, [(0, load), (3, store)])
            for k in range(2):
                e.wait_ge(s_o[k], 16 * len(range(k, NG, 2)))

        @blk.tensor
        def _(e):
            e.wait_ge(w, 64)

            def mm(g):
                c, n, nb = cols(g)
                q = g % 2
                if g >= 2:
                    e.wait_ge(s_f[0], g - 1)
                if g >= 1:
                    e.wait_ge(s_f[0], g)
                for b in range(nb):
                    cc = slice(c.start + b * 128, c.start + (b + 1) * 128)
                    for h in range(2):
                        e.matmul(H[h][q][:, b * 128:(b + 1) * 128], acc[:, 1 + h, cc], gw[:, h * 128:(h + 1) * 128],
                                 start=True, stop=True)
                        m = e.matmul(DN[:, 2 * b + h:2 * b + h + 1], acc[32:33, 3 + h, cc], ones[32:33, 0:1],
                                     start=True, stop=True)
                m.then_inc(s_mm, 1)

            steps(NG, [(0, mm)])

        @blk.vector
        def _(e):
            ch = Chain(e, s_v)
            e.wait_ge(w, 64)

            def stats(g, k, src):
                nb, q = cols(g)[2], g % 2
                for b in range(nb):
                    ch(e.bn_stats(bn[:, b, :], src[:, q, b, :]))
                ch.sync()
                for b in range(nb):
                    ch(e.bn_aggr(mv[:, k, q, b, :], bn[:, b, :]))
                ch.sync()
                ch(e.tensor_scalar(rs[:, k, q, 0:nb], mv[:, k, q, 0:nb, 1], EPS, None, ALU.add))
                ch.raises(s_f[k])

            def norm(g, k, src, dst):
                nb, q = cols(g)[2], g % 2
                e.wait_ge(s_rs[k], g + 1)
                ch(e.reciprocal(rs[:, k, q, 0:nb], rs[:, k, q, 0:nb]))
                ch.sync()
                for b in range(nb):
                    ch(e.tensor_scalar(dst[:, q, b, :], src[:, q, b, :], mv[:, k, q, b, 0:1], rs[:, k, q, b:b + 1],
                                       ALU.subtract, ALU.mult))
                ch.sync()

            def f1(g):
                c, n, nb = cols(g)
                q = g % 2
                e.wait_ge(s_mm, g + 1)
                ch(e.tensor_scalar(rd[:, q, 0:2 * nb], DN[:, 0:2 * nb], 2.0, None, ALU.mult))
                ch.sync()
                ch(e.reciprocal(rd[:, q, 0:2 * nb], rd[:, q, 0:2 * nb]))
                ch.sync()
                for h, add in ((0, gb[:, 0, :]), (1, None)):
                    for b in range(nb):
                        ch(e.scalar_tensor_tensor(tt[:, q, b, :], H[h][q][:, b * 128:(b + 1) * 128],
                                                  rd[:, q, 2 * b + h:2 * b + h + 1], tt[:, q, b, :] if h else add,
                                                  ALU.mult, ALU.add))
                    ch.sync()
                stats(g, 0, tt)

            def f2(g):
                nb, q = cols(g)[2], g % 2
                norm(g, 0, tt, tt)
                bc = lambda k: gb[:, k:k + 1, :].to_broadcast([128, nb, 128])
                ch(e.tensor_tensor(tt[:, q, 0:nb, :], tt[:, q, 0:nb, :], bc(1), ALU.mult))
                ch.sync()
                ch(e.tensor_tensor(zz[:, q, 0:nb, :], tt[:, q, 0:nb, :], bc(2), ALU.add))
                ch.raises(s_z)

            def f3(g):
                nb, q = cols(g)[2], g % 2
                e.wait_ge(s_h, g + 1)
                e.wait_ge(s_x[q], 16 * (g // 2 + 1))
                ch(e.tensor_tensor(yy[:, q, 0:nb, :], zz[:, q, 0:nb, :], x1[:, q, 0:nb, :], ALU.add))
                ch.raises(s_y)
                stats(g, 1, yy)

            def f4(g):
                q = g % 2
                if g >= 2:
                    e.wait_ge(s_o[q], 16 * (g // 2))
                norm(g, 1, yy, oo)
                e.engine_nop().then_inc(s_out, 1)

            steps(NG, [(2, f3), (3, f4), (1, f2), (0, f1)])

        @blk.scalar
        def _(e):
            def root(k):
                def f(g):
                    nb, q = cols(g)[2], g % 2
                    e.wait_ge(s_f[k], g + 1)
                    e.activation(rs[:, k, q, 0:nb], rs[:, k, q, 0:nb], ACT.Sqrt).then_inc(s_rs[k], 1)
                return f

            def h(g):
                nb, q = cols(g)[2], g % 2
                e.wait_ge(s_z, g + 1)
                e.activation(zz[:, q, 0:nb, :], zz[:, q, 0:nb, :], ACT.Silu).then_inc(s_h, 1)

            steps(NG, [(2, root(1)), (1, h), (0, root(0))])


def lay_out(x, src, dst, edge_attr_64, np):
    pad = EP - E
    src = np.concatenate([np.asarray(src), np.zeros(pad, np.int32)])
    dst = np.concatenate([np.asarray(dst), np.full(pad, N, np.int32)])
    minus = np.full(1, -1, np.int32)
    lin = np.concatenate([minus, dst, minus])
    chunks = lambda a: a.reshape(NCH, 4, 128)
    a = {
        "xT": np.concatenate([np.asarray(x).T, np.zeros((128, NP - N), np.float32)], axis=1),
        "lin": lin,
        "meta": np.concatenate([chunks(x).transpose(0, 2, 1) for x in (src, dst, lin[2:])], axis=2),
        "eft": np.concatenate([np.asarray(edge_attr_64).T, np.zeros((64, pad), np.float32)], axis=1),
    }
    return a


def arrays_of(np, i):
    a = lay_out(i["x"], i["src"], i["dst"], i["edge_attr_64"], np)
    g = lambda n: np.asarray(i[n])
    a["wpre"] = g("L0_gnn_W_pre")
    a["bpre"] = g("L0_gnn_b_pre")
    a["w1"] = g("L0_gnn_W_post1")
    a["b1"] = g("L0_gnn_b_post1").reshape(128, 1)
    a["w2"] = g("L0_gnn_W_post2")
    a["b2"] = g("L0_gnn_b_post2").reshape(128, 1)
    a["gcnw"] = g("L1_gnn_gcn_w")
    a["gcnb"] = g("L1_gnn_gcn_b")
    a["gatw"] = g("L1_gnn_gat_w")
    a["gatwT"] = g("L1_gnn_gat_w").T
    a["atts"] = g("L1_gnn_att_src").T
    a["attd"] = g("L1_gnn_att_dst").T
    a["gatb"] = g("L1_gnn_gat_b")
    a["gamma"] = g("L1_gnn_ln_gamma")
    a["beta"] = g("L1_gnn_ln_beta")
    return {k: np.ascontiguousarray(x) for k, x in a.items()}


def make(nc, arrays, upto=99):
    d = {k: nc.dram_tensor("in_" + k, x.shape, mybir.dt.from_np(x.dtype), kind="ExternalInput").ap()
         for k, x in arrays.items()}
    out = nc.dram_tensor("out_0_dram", (N, 128), F32, kind="ExternalOutput").ap()
    build(nc, d, out, upto)


def kernel(**inputs):
    import numpy as np
    import concourse.bacc as bacc
    from concourse.bass_utils import run_bass_kernel_spmd as run

    arrays = arrays_of(np, inputs)
    nc = bacc.Bacc("TRN2", target_bir_lowering=False, num_devices=1)
    make(nc, arrays)
    r = run(nc, [{"in_" + k: x for k, x in arrays.items()}], core_ids=[0])
    return r.results[0]["out_0_dram"]
```

```python
from contextlib import ExitStack

import concourse.bass as bass
from concourse import mybir

F32 = mybir.dt.float32
BF16 = mybir.dt.bfloat16
I32 = mybir.dt.int32
ALU = mybir.AluOpType
ACT = mybir.ActivationFunctionType
ds = bass.ds

N = 6250
E = 206250
NP = 6400
NB = NP // 128
CH = 512
NCH = (E + CH - 1) // CH
EP = NCH * CH
COLS = EP // 128
W = 64
TMAX = 640
TJ = TMAX // 128
TK = 2 * TMAX + 24
TLESS = 64
BIG = 1.0e30
EPS = 1e-5
GROUPS = [(g * 512, min(512, NP - g * 512)) for g in range((NP + 511) // 512)]


class Entry:

    def __init__(self, i, o):
        self.i, self.o = i, o

    def at(self, n=0):
        return self.i + (self.o + n)

    def slot(self, m):
        return self.o % m

    def uses(self, m, n=0):
        return (self.i + (self.o + m * (1 + n))) // m

    def first(self, m):
        return isinstance(self.i, int) and self.i + self.o < m


def pipeline(eng, T, U, D, stages):
    for i in range(D):
        for lag, f in stages:
            if i >= lag:
                f(Entry(i // U * U, i % U - lag))
    with eng.bass.Fori(D, T, U, engines=bass.OrderedEngineSet([eng.engine])) as i:
        for k in range(U):
            for lag, f in stages:
                f(Entry(i, k - lag))
    for k in range(D):
        for lag, f in stages:
            if k < lag:
                f(Entry(T, k - lag))


class Chain:

    def __init__(self, eng, sem):
        self.eng, self.sem, self.n = eng, sem, 0

    def __call__(self, ins):
        self.n += 1
        return ins.then_inc(self.sem, 1)

    def sync(self):
        self.eng.wait_ge(self.sem, self.n)

    def raises(self, sem):
        self.sync()
        self.eng.engine_nop().then_inc(sem, 1)


def build(nc, d, out, upto=99):
    with ExitStack() as top:
        def sem(name):
            return top.enter_context(nc.semaphore(name))

        def sbt(stack, name, shape, dt=F32):
            return stack.enter_context(nc.sbuf_tensor(name, shape, dt))

        def pst(stack, name, shape, dt=F32):
            return stack.enter_context(nc.psum_tensor(name, shape, dt))

        def dram(name, shape, dt=F32):
            return nc.dram_tensor(name, shape, dt).ap()

        Atab = dram("Atab", [NP, 128])
        Btab = dram("Btab", [NP, 128])
        MM = dram("MM", [2, EP], BF16)
        TBI = dram("TBI", [2 * TMAX], I32)
        TBF = dram("TBF", [TMAX], F32)
        X1D = dram("X1D", [NP, 128])
        XS = dram("XS", [NP, 128])
        TAB = dram("TAB", [NP, 130])
        ADT = dram("ADT", [NP, 2])
        DQ = dram("DQ", [3, NP])
        DEG = dram("DEG", [NP])

        acc = sbt(top, "acc", [128, 5, NP])
        baseF = sbt(top, "baseF", [128, TMAX + 16])
        tb = sbt(top, "tb", [1, 2 * TMAX + 64], I32)
        ident = sbt(top, "ident", [128, 128])
        iotaW = sbt(top, "iotaW", [128, W])
        nid = sbt(top, "nid", [128, 1])
        ones = sbt(top, "ones", [128, 128])
        dinv = sbt(top, "dinv", [128, NB])
        onesb = sbt(top, "onesb", [128, 128], BF16)

        s_pool = sem("s_pool")
        s_sync = sem("s_sync")
        s_pad = sem("s_pad")

        with ExitStack() as ph:
            xT = acc[:, 0, :]
            wsd = sbt(ph, "wsd", [128, 2, 128])
            bpre = sbt(ph, "bpre", [128, 128])
            stg = sbt(ph, "stg", [128, 2, 5, 256])
            dn = sbt(ph, "dn", [128, COLS], I32)
            dp = sbt(ph, "dp", [128, COLS], I32)
            mk = sbt(ph, "mk", [128, COLS], BF16)
            mk2 = sbt(ph, "mk2", [128, COLS], BF16)
            rows = sbt(ph, "rows", [1, 8, NCH + 1])
            rowi = sbt(ph, "rowi", [1, 2, NCH + 1], I32)
            ob = sbt(ph, "ob", [128, 2, NCH])
            iotaC = sbt(ph, "iotaC", [128, NCH])
            tcol = sbt(ph, "tcol", [128, TJ])
            ends = sbt(ph, "ends", [128, len(GROUPS) - 1])
            early = sbt(ph, "early", [128, len(GROUPS) - 1, TJ])
            seg = sbt(ph, "seg", [1, 4, len(GROUPS)])
            segi = sbt(ph, "segi", [1, len(GROUPS)], I32)
            tmp = sbt(ph, "tmp", [128, 2, NCH])
            cols = sbt(ph, "cols", [128, 6])
            tabf = sbt(ph, "tabf", [128, 2, TJ])
            tabi = sbt(ph, "tabi", [128, 2, TJ], I32)
            pw = [pst(ph, f"pw{k}", [128, 512]) for k in range(4)]
            pb = [pst(ph, f"pb{k}", [128, 512]) for k in range(2)]
            p_in = sem("p_in")
            p_idx = sem("p_idx")
            p_row = sem("p_row")
            p_c = sem("p_c")
            p_mm = sem("p_mm")
            p_ev = sem("p_ev")
            p_x = [sem("p_x0"), sem("p_x1")]
            p_z = sem("p_z")
            p_e = sem("p_e")
            p_es = sem("p_es")
            p_out = [sem("p_out0"), sem("p_out1")]
            p_d = sem("p_d")
            p_bc = sem("p_bc")
            p_rw = sem("p_rw")
            p_msk = sem("p_msk")
            p_tab = sem("p_tab")
            p_fin = sem("p_fin")
            blk = ph.enter_context(nc.Block())

            @blk.sync
            def _(e):
                e.dma_start(wsd[:, 0, :], d["wpre"][0:128, :]).then_inc(p_in, 16)
                e.dma_start(wsd[:, 1, :], d["wpre"][128:256, :]).then_inc(p_in, 16)
                for k in range(2):
                    c = slice(k * NP // 2, (k + 1) * NP // 2)
                    e.dma_start(xT[:, c], d["xT"][:, c]).then_inc(p_x[k], 16)
                    if k == 0:
                        e.wait_ge(p_c, 9)
                        e.dma_start(bpre[0:1, :], d["bpre"].rearrange("(a n) -> a n", a=1)).then_inc(p_in, 16)
                for g in range(NB // 5):
                    e.wait_ge(p_ev, 5 * (g + 1))
                    for t, o in ((Atab, 0), (Btab, 128)):
                        e.dma_start(t[g * 640:(g + 1) * 640, :].rearrange("(b p) f -> p b f", p=128),
                                    stg[:, g % 2, :, o:o + 128]).then_inc(p_out[g % 2], 16)
                e.wait_ge(p_out[0], 16 * 2 * 5)
                e.wait_ge(p_out[1], 16 * 2 * 5)

            @blk.gpsimd
            def _(e):
                e.memset(ident[:, :], 0.0).then_inc(p_c, 1)
                e.wait_ge(p_c, 1)
                e.affine_select(out=ident[:, :], in_=ident[:, :], compare_op=ALU.not_equal, fill=1.0,
                                base=0, pattern=[[-1, 128]], channel_multiplier=1).then_inc(p_c, 1)
                e.memset(ones[:, :], 1.0).then_inc(p_c, 1)
                e.memset(onesb[:, :], 1.0).then_inc(p_c, 1)
                e.iota(iotaW[:, :], pattern=[[1, W]], base=0, channel_multiplier=0,
                       allow_small_or_imprecise_dtypes=True).then_inc(p_c, 1)
                e.iota(cols[:, 5:6], pattern=[[0, 1]], base=0, channel_multiplier=1,
                       allow_small_or_imprecise_dtypes=True).then_inc(p_c, 1)
                e.iota(iotaC[:, :], pattern=[[1, NCH]], base=0, channel_multiplier=0,
                       allow_small_or_imprecise_dtypes=True).then_inc(p_c, 1)
                e.iota(tcol[:, :], pattern=[[128, TJ]], base=0, channel_multiplier=1,
                       allow_small_or_imprecise_dtypes=True).then_inc(p_c, 1)
                e.memset(bpre[:, :], 0.0).then_inc(p_c, 1)
                e.iota(ends[:, :], pattern=[[512, len(GROUPS) - 1]], base=512, channel_multiplier=0,
                       allow_small_or_imprecise_dtypes=True).then_inc(p_c, 1)
                e.memset(acc[:, 1:5, :], 0.0).then_inc(p_z, 1)
                e.wait_ge(p_msk, 2)
                e.dma_start(MM[0, :].rearrange("(p t) -> p t", p=128), mk[:, :]).then_inc(p_fin, 16)
                e.dma_start(MM[1, :].rearrange("(p t) -> p t", p=128), mk2[:, :]).then_inc(p_fin, 16)
                e.wait_ge(p_tab, 2)
                e.dma_start(TBI.rearrange("(k j p) -> p k j", k=2, p=128), tabi[:, :, :], allow_slow_non_contiguous=True).then_inc(p_fin, 16)
                e.dma_start(TBF.rearrange("(j p) -> p j", p=128), tabf[:, 1, :], allow_slow_non_contiguous=True).then_inc(p_fin, 16)
                e.wait_ge(p_fin, 64)
                e.dma_start(tb[0:1, 0:2 * TMAX], TBI.rearrange("(a n) -> a n", a=1)).then_inc(p_fin, 16)
                e.dma_start(baseF[:, 0:TMAX], TBF.partition_broadcast(128)).then_inc(p_fin, 16)
                e.wait_ge(p_fin, 96)

            @blk.tensor
            def _(e):
                e.wait_ge(p_in, 48)
                e.wait_ge(p_c, 3)
                for b in range(NB):
                    e.wait_ge(p_x[2 * b // NB], 16)
                    if b >= 4:
                        e.wait_ge(p_ev, b - 3)
                    t = pw[b % 4]
                    xb = xT[:, b * 128:(b + 1) * 128]
                    e.matmul(t[:, 0:128], xb, wsd[:, 0, :], start=True, stop=True)
                    e.matmul(t[:, 128:256], xb, wsd[:, 1, :], start=True, stop=False)
                    e.matmul(t[:, 128:256], ones[:, :], bpre[:, :], start=False, stop=True).then_inc(p_mm, 1)
                    if b == 0:
                        e.wait_ge(p_rw, 1)
                        for k in range(2):
                            e.matmul(pb[k][:, 0:NCH], ones[0:1, :], rows[0:1, k, 0:NCH],
                                     start=True, stop=True).then_inc(p_bc, 1)
                    if b == 40:
                        e.wait_ge(p_e, 1)
                        e.matmul(pb[0][0:1, 0:(len(GROUPS) - 1) * TJ], ones[:, 0:1],
                                 early[:, :, :].rearrange("p g j -> p (g j)"), start=True, stop=True).then_inc(p_es, 1)

            @blk.scalar
            def _(e):
                for k in range(2):
                    e.dma_start(rowi[0:1, k, 0:NCH],
                                d["lin"][1:1 + EP].rearrange("(a c b) -> a c b", a=1, b=CH)[:, :, k * (CH - 1)],
                                allow_slow_non_contiguous=True).then_inc(p_row, 16)
                e.dma_start(dn[:, :], d["lin"][1:1 + EP].rearrange("(p t) -> p t", p=128)).then_inc(p_idx, 16)
                e.dma_start(dp[:, :], d["lin"][0:EP].rearrange("(p t) -> p t", p=128)).then_inc(p_idx, 16)
                for b in range(NB):
                    g = b // 5
                    e.wait_ge(p_mm, b + 1)
                    if b % 5 == 0 and g >= 2:
                        e.wait_ge(p_out[g % 2], 32 * (g // 2))
                    e.copy(stg[:, g % 2, b % 5, :], pw[b % 4][:, 0:256]).then_inc(p_ev, 1)

            @blk.vector
            def _(e):
                ch = Chain(e, p_d)
                R = lambda k: rows[0:1, k, 0:NCH]
                e.wait_ge(p_row, 32)
                ch(e.tensor_copy(R(1), rowi[0:1, 0, 0:NCH]))
                ch(e.tensor_copy(R(2), rowi[0:1, 1, 0:NCH]))
                ch(e.memset(R(6), 1.0))
                ch.sync()
                ch(e.tensor_tensor(rowi[0:1, 0, 0:NCH], R(2), R(1), ALU.subtract))
                ch.sync()
                ch(e.tensor_scalar(rowi[0:1, 1, 0:NCH], rowi[0:1, 0, 0:NCH], 6, None, ALU.arith_shift_right))
                ch.sync()
                ch(e.tensor_scalar(R(4), rowi[0:1, 1, 0:NCH], 1.0, None, ALU.add))
                ch.sync()
                ch(e.tensor_tensor_scan(R(5), R(6), R(4), 0.0, ALU.mult, ALU.add))
                ch.sync()
                ch(e.tensor_tensor(R(0), R(5), R(4), ALU.subtract))
                ch.sync()
                for k, m in ((0, 2), (1, 3)):
                    o = rowi[0:1, 0, k:k + 1]
                    ch(e.tensor_scalar(o, rows[0:1, 5, NCH - 1:NCH], float(2 ** m - 1), None, ALU.add))
                    ch.sync()
                    ch(e.tensor_scalar(o, o, m, m, ALU.arith_shift_right, ALU.arith_shift_left))
                    ch.sync()
                    ch(e.tensor_scalar(tb[0:1, TK + k:TK + k + 1], o, float(-TLESS), None, ALU.add))
                ch.sync()
                e.engine_nop().then_inc(p_rw, 1)
                e.wait_ge(p_bc, 2)
                e.wait_ge(p_c, 8)
                ch(e.tensor_scalar(cols[:, 4:5], cols[:, 5:6], float(W), float(-W), ALU.is_ge, ALU.mult))
                ch.sync()
                ch(e.tensor_tensor(nid[:, :], cols[:, 5:6], cols[:, 4:5], ALU.add))
                ch(e.tensor_copy(ob[:, 0, :], pb[0][:, 0:NCH]))
                ch(e.tensor_copy(ob[:, 1, :], pb[1][:, 0:NCH]))
                ch.sync()
                for j in range(TJ):
                    t = tcol[:, j:j + 1]
                    ch(e.tensor_scalar(tmp[:, 0, :], ob[:, 0, :], t, None, ALU.is_le))
                    ch.sync()
                    ch(e.tensor_reduce(cols[:, 0:1], tmp[:, 0, :], mybir.AxisListType.X, ALU.add))
                    ch.sync()
                    ch(e.tensor_scalar(tabf[:, 0, j:j + 1], cols[:, 0:1], -1.0, None, ALU.add))
                    ch.sync()
                    ch(e.tensor_scalar(tmp[:, 0, :], iotaC[:, :], tabf[:, 0, j:j + 1], None, ALU.is_equal))
                    ch.sync()
                    for k in range(2):
                        ch(e.tensor_tensor(tmp[:, 1, :], tmp[:, 0, :], ob[:, k, :], ALU.mult))
                        ch.sync()
                        ch(e.tensor_reduce(cols[:, 1 + k:2 + k], tmp[:, 1, :], mybir.AxisListType.X, ALU.add))
                        ch.sync()
                    ch(e.tensor_tensor(cols[:, 3:4], t, cols[:, 1:2], ALU.subtract))
                    ch.sync()
                    ch(e.tensor_scalar(cols[:, 4:5], cols[:, 3:4], float(W), cols[:, 2:3], ALU.mult, ALU.add))
                    ch.sync()
                    ch(e.tensor_scalar(tabf[:, 1, j:j + 1], cols[:, 4:5], float(N), None, ALU.min))
                    ch.sync()
                e.tensor_copy(tabi[:, :, :], tabf[:, :, :]).then_inc(p_tab, 1)
                e.engine_nop().then_inc(p_tab, 1)
                n = len(GROUPS)
                e.wait_ge(p_c, 10)
                ch.sync()
                e.wait_ge(p_tab, 2)
                e.tensor_tensor(early[:, :, :], tabf[:, 1:2, :].to_broadcast([128, n - 1, TJ]),
                                ends[:, :].unsqueeze(2).to_broadcast([128, n - 1, TJ]), ALU.is_lt).then_inc(p_e, 1)
                e.wait_ge(p_es, 1)
                ch(e.tensor_reduce(seg[0:1, 0, 0:n - 1], pb[0][0:1, 0:(n - 1) * TJ].rearrange("p (g j) -> p g j", g=n - 1),
                                   mybir.AxisListType.X, ALU.add))
                ch(e.tensor_copy(seg[0:1, 0, n - 1:n], rows[0:1, 5, NCH - 1:NCH]))
                ch(e.memset(seg[0:1, 1, :], 4.0))
                ch.sync()
                ch(e.tensor_scalar(segi[:, :], seg[0:1, 0, :], 3.0, None, ALU.add))
                ch.sync()
                ch(e.tensor_scalar(segi[:, :], segi[:, :], 2, 2, ALU.arith_shift_right, ALU.arith_shift_left))
                ch.sync()
                ch(e.tensor_copy(seg[0:1, 2, :], segi[:, :]))
                ch.sync()
                ch(e.tensor_tensor_scan(seg[0:1, 3, :], seg[0:1, 1, :], seg[0:1, 2, :], 4.0, ALU.add, ALU.max))
                ch.sync()
                ch(e.tensor_scalar(tb[0:1, TK + 2:TK + 2 + n], seg[0:1, 3, :], -4.0, None, ALU.add))
                e.wait_ge(p_idx, 32)
                e.tensor_tensor(mk[:, :], dn[:, :], dp[:, :], ALU.is_equal).then_inc(p_msk, 1)
                ch(e.tensor_tensor(mk2[:, :], dn[:, :], dp[:, :], ALU.not_equal))
                ch.sync()
                e.tensor_scalar(mk2[:, :], mk2[:, :], BIG, None, ALU.mult).then_inc(p_msk, 1)
                for b in range(0, NB, 10):
                    e.wait_ge(p_mm, b + 10)
                    ch(e.memset(acc[:, 0, b * 128:(b + 10) * 128], 0.0))
                ch.sync()
                e.wait_ge(p_z, 1)
        if upto < 1:
            return
        phase_l0(nc, d, locals())
        if upto < 2:
            return
        phase_n1(nc, d, locals())
        if upto < 3:
            return
        phase_gcn(nc, d, locals())
        if upto < 5:
            return
        phase_gat(nc, d, locals())
        phase_n3(nc, d, locals(), out)


def wait(e, s, v):
    if not isinstance(v, int) or v > 0:
        e.wait_ge(s, v)


def keep(e, regs, j, b):
    e.reg_mov(regs[j.slot(len(regs))], b)
    return b


def kept(e, regs, j):
    return e.snap(regs[j.slot(len(regs))], min_val=0, max_val=N)


def wait_sync(e, s, v, pad):
    e.wait_ge(s, v)
    e.sem_inc(pad, 1)


def load_T(e, tb, k):
    return e.value_load(tb[0:1, TK + k:TK + k + 1], min_val=NCH - TLESS, max_val=TMAX - TLESS) + TLESS


def load_end(e, tb, g):
    return e.value_load(tb[0:1, TK + 2 + g:TK + 3 + g], min_val=0, max_val=TMAX - 4) + 4


def chunk_of(e, tb, j):
    return e.value_load(tb[0:1, ds(j.at(), 1)], min_val=0, max_val=NCH - 1)


def base_of(e, tb, j):
    return e.value_load(tb[0:1, ds(j.at() + TMAX, 1)], min_val=0, max_val=N)


def phase_l0(nc, d, v):
    sem, sbt, pst = v["sem"], v["sbt"], v["pst"]
    acc, baseF, tb = v["acc"], v["baseF"], v["tb"]
    ident, iotaW, nid, onesb = v["ident"], v["iotaW"], v["nid"], v["onesb"]
    Atab, Btab, MM = v["Atab"], v["Btab"], v["MM"]
    with ExitStack() as ph:
        meta = sbt(ph, "meta", [128, 4, 12], I32)
        ZR = sbt(ph, "ZR", [128, 4, CH])
        WB = sbt(ph, "WB", [128, 4, 128])
        dstb = sbt(ph, "dstb", [128, 4, CH], I32)
        mm2 = sbt(ph, "mm2", [128, 4, 2, CH], BF16)
        G = sbt(ph, "G", [128, 4, 4, 128])
        EE = sbt(ph, "EE", [128, 2, 2, CH])
        oh = sbt(ph, "oh", [128, 4, 4, W])
        ohb = sbt(ph, "ohb", [128, 2, 4, W], BF16)
        ohl = sbt(ph, "ohl", [128, 4, 4, W])
        neq = sbt(ph, "neq", [128, 4, 4])
        iob = sbt(ph, "iob", [128, 2, W])
        ST = sbt(ph, "ST", [128, 2, 2, CH])
        BS = sbt(ph, "BS", [128, 2, 2, CH])
        Z = [pst(ph, f"Z{k}", [128, CH]) for k in range(2)]
        ET = [pst(ph, f"ET{k}", [128, CH]) for k in range(2)]
        S1 = pst(ph, "S1", [128, 512])
        S2 = pst(ph, "S2", [128, 512])
        BK = [pst(ph, f"BK{k}", [128, CH]) for k in range(2)]
        S1v = S1[:, 0:3 * W].rearrange("p (a n) -> p a n", a=3)
        S2v = S2[:, 0:2 * W].rearrange("p (a n) -> p a n", a=2)
        l_we = sem("l_we")
        l_mt = [sem(f"l_mt{k}") for k in range(4)]
        l_in = [sem(f"l_in{k}") for k in range(4)]
        l_db = [sem(f"l_db{k}") for k in range(4)]
        l_m = [sem(f"l_m{k}") for k in range(4)]
        l_g = [sem(f"l_g{k}") for k in range(4)]
        s_iob = sem("l_iob")
        s_zr = sem("l_zr")
        s_d1 = sem("l_d1")
        s_p1 = sem("l_p1")
        s_d2 = sem("l_d2")
        s_r = sem("l_r")
        s_a1 = sem("l_a1")
        s_p2 = sem("l_p2")
        s_p2t = sem("l_p2t")
        s_d3 = sem("l_d3")
        s_ohl = sem("l_ohl")
        s_p3 = sem("l_p3")
        s_a2 = sem("l_a2")
        s_p4 = sem("l_p4")
        s_d4a = sem("l_d4a")
        s_d4b = sem("l_d4b")
        s_i = sem("l_i")
        s_pool = v["s_pool"]
        s_pad = v["s_pad"]
        s_sync = v["s_sync"]
        blk = ph.enter_context(nc.Block())
        U, D = 4, 8

        @blk.sync
        def _(e):
            for k in range(4):
                e.dma_start(WB[0:64, k, :], d["wpre"][256:320, :]).then_inc(l_we, 16)
            T = load_T(e, tb, 0)

            def loads(j):
                c, b = chunk_of(e, tb, j), base_of(e, tb, j)
                k = j.slot(4)
                e0 = c * CH
                src = (d["meta"][ds(c, 1), :, :].rearrange("a p s -> (a p) s"), d["eft"][:, ds(e0, CH)],
                       Btab[ds(b, 64), :], d["lin"][ds(e0 + 1, CH)].partition_broadcast(64))
                before = 64 * j.uses(4, -1), j.at(-3)
                if not j.first(4):
                    wait_sync(e, l_g[k], before[0], s_sync)
                    wait_sync(e, s_d1, before[1], s_sync)
                e.dma_start(meta[:, k, :], src[0]).then_inc(l_mt[k], 16)
                if not j.first(4):
                    wait_sync(e, s_p1, before[1], s_sync)
                e.dma_start(ZR[0:64, k, :], src[1]).then_inc(l_in[k], 16)
                e.dma_start(WB[64:128, k, :], src[2]).then_inc(l_in[k], 16)
                e.dma_start(dstb[64:128, k, :], src[3]).then_inc(l_db[k], 16)

            pipeline(e, T, U, D, [(0, loads)])

        @blk.gpsimd
        def _(e):
            T = load_T(e, tb, 0)

            def gather(j):
                k = j.slot(4)
                wait(e, l_mt[k], 16 * j.uses(4))
                if not j.first(4):
                    wait(e, s_d2, j.at(-3))
                e.sem_inc(s_pool, 1)
                for s in range(4):
                    e.indirect_dma_start(G[:, k, s, :], None, Atab,
                                         bass.IndirectOffsetOnAxis(ap=meta[:, k, s:s + 1], axis=0)).then_inc(l_g[k], 16)

            pipeline(e, T, U, D, [(0, gather)])

        @blk.vector
        def _(e):
            e.memset(ST[:, :, :, :], 0.0).then_inc(s_i, 1)
            e.wait_ge(s_i, 1)
            T = load_T(e, tb, 0)

            def d1(j):
                k, q = j.slot(4), j.slot(2)
                e.tensor_scalar(iob[:, q, :], iotaW[:, :], baseF[:, ds(j.at(), 1)], None, ALU.add).then_inc(s_iob, 1)
                wait(e, l_db[k], 16 * j.uses(4))
                if not j.first(4):
                    wait(e, s_p1, j.at(-3))
                e.tensor_scalar(ZR[64:128, k, :], dstb[64:128, k, :], baseF[64:128, ds(j.at(), 1)], nid[64:128, 0:1],
                                ALU.subtract, ALU.is_equal).then_inc(s_zr, 1)
                wait(e, l_mt[k], 16 * j.uses(4))
                if not j.first(4):
                    wait(e, s_ohl, j.at(-3))
                e.tensor_tensor(neq[:, k, :], meta[:, k, 4:8], meta[:, k, 8:12], ALU.not_equal)
                if not j.first(4):
                    wait(e, s_p2, j.at(-3))
                wait(e, s_iob, j.at(1))
                e.tensor_tensor(oh[:, k, :, :], iob[:, q:q + 1, :].to_broadcast([128, 4, W]),
                                meta[:, k, 4:8].unsqueeze(2).to_broadcast([128, 4, W]),
                                ALU.is_equal).then_inc(s_d1, 1)

            def d2(j):
                wait(e, s_p1, j.at(1))
                wait(e, l_g[j.slot(4)], 64 * j.uses(4))
                if not j.first(2):
                    wait(e, s_p2, j.at(-1))
                e.tensor_tensor(EE[:, j.slot(2), 1, :], Z[j.slot(2)][:, :],
                                G[:, j.slot(4), :, :].rearrange("p s f -> p (s f)"), ALU.add).then_inc(s_d2, 1)

            def last(j):
                k = j.slot(4)
                if not j.first(4):
                    wait(e, s_p4, j.at(-3))
                wait(e, s_d1, j.at(1))
                e.tensor_tensor(ohl[:, k, :, :], oh[:, k, :, :], neq[:, k, :].unsqueeze(2).to_broadcast([128, 4, W]),
                                ALU.mult).then_inc(s_ohl, 1)

            def d3(j):
                k, q = j.slot(4), j.slot(2)
                wait(e, s_p2t, j.at(1))
                wait(e, l_m[k], 16 * j.uses(4))
                if not j.first(2):
                    wait(e, s_p3, j.at(-1))
                if not j.first(1):
                    wait(e, s_d3, j.at())
                e.tensor_tensor_scan(ST[:, q, 0, :], mm2[:, k, 0, :], ET[q][:, :], ST[:, 1 - q, 0, CH - 1:CH],
                                     ALU.mult, ALU.max)
                e.tensor_tensor_scan(ST[:, q, 1, :], mm2[:, k, 1, :], ET[q][:, :], ST[:, 1 - q, 1, CH - 1:CH],
                                     ALU.max, ALU.min).then_inc(s_d3, 1)

            regs = [e.alloc_register(f"l_base{k}") for k in range(4)]

            def d4(j, S, n, lo, s_in, s_out, b):
                wait(e, s_in, j.at(1))
                if not j.first(1):
                    wait(e, s_out, j.at())
                a = acc[:, lo:lo + n, ds(b, W)]
                e.tensor_tensor(a, a, S, ALU.add).then_inc(s_out, 1)

            def d4a(j):
                d4(j, S1v, 3, 0, s_p2, s_d4a, keep(e, regs, j, base_of(e, tb, j)))

            def d4b(j):
                d4(j, S2v, 2, 3, s_p4, s_d4b, kept(e, regs, j))

            pipeline(e, T, U, D, [(7, d4b), (2, d2), (0, d1), (3, last), (4, d4a), (4, d3)])

        @blk.scalar
        def _(e):
            T = load_T(e, tb, 0)

            def a1(j):
                q = j.slot(2)
                wait(e, s_d1, j.at(1))
                if not j.first(2):
                    wait(e, s_p2, j.at(-1))
                e.copy(ohb[:, q, :, :], oh[:, j.slot(4), :, :])
                wait(e, s_d2, j.at(1))
                e.activation(EE[:, q, 0, :], EE[:, q, 1, :], ACT.Relu).then_inc(s_r, 1)
                wait(e, s_r, j.at(1))
                e.activation(EE[:, q, 1, :], EE[:, q, 0, :], ACT.Square).then_inc(s_a1, 1)

            def masks(j):
                c = chunk_of(e, tb, j)
                k = j.slot(4)
                if not j.first(4):
                    wait(e, s_d3, j.at(-3))
                    e.sem_inc(s_pad, 1)
                e.dma_start(mm2[:, k, :, :], MM[:, ds(c * CH, CH)].partition_broadcast(128)).then_inc(l_m[k], 16)

            def a2(j):
                q = j.slot(2)
                wait(e, s_p3, j.at(1))
                if not j.first(2):
                    wait(e, s_p4, j.at(-1))
                e.copy(BS[:, q, 0, :], BK[0][:, :])
                e.copy(BS[:, q, 1, :], BK[1][:, :]).then_inc(s_a2, 1)

            pipeline(e, T, U, D, [(5, a2), (1, masks), (2, a1)])

        @blk.tensor
        def _(e):
            e.wait_ge(l_we, 64)
            T = load_T(e, tb, 0)

            def p1(j):
                q, k = j.slot(2), j.slot(4)
                wait(e, s_zr, j.at(1))
                wait(e, l_in[k], 32 * j.uses(4))
                if not j.first(2):
                    wait(e, s_d2, j.at(-1))
                for s in range(4):
                    mm = e.matmul(Z[q][:, s * 128:(s + 1) * 128], ZR[:, k, s * 128:(s + 1) * 128], WB[:, k, :],
                                  start=True, stop=True)
                mm.then_inc(s_p1, 1)

            def p2(j):
                q, k = j.slot(2), j.slot(4)
                wait(e, s_a1, j.at(1))
                if not j.first(2):
                    wait(e, s_d3, j.at(-1))
                for s in range(4):
                    mm = e.transpose(ET[q][:, s * 128:(s + 1) * 128], EE[:, q, 0, s * 128:(s + 1) * 128], ident[:, :])
                mm.then_inc(s_p2t, 1)
                if not j.first(1):
                    wait(e, s_d4a, j.at())
                for a in range(3):
                    for s in range(4):
                        lhs = EE[:, q, a, s * 128:(s + 1) * 128] if a < 2 else onesb[:, :]
                        rhs = oh[:, k, s, :] if a < 2 else ohb[:, q, s, :]
                        mm = e.matmul(S1[:, a * W:(a + 1) * W], lhs, rhs, start=(s == 0), stop=(s == 3))
                mm.then_inc(s_p2, 1)

            def p3(j):
                q = j.slot(2)
                wait(e, s_d3, j.at(1))
                if not j.first(1):
                    wait(e, s_a2, j.at())
                for a in range(2):
                    for s in range(4):
                        mm = e.transpose(BK[a][:, s * 128:(s + 1) * 128], ST[:, q, a, s * 128:(s + 1) * 128], ident[:, :])
                mm.then_inc(s_p3, 1)

            def p4(j):
                q, k = j.slot(2), j.slot(4)
                wait(e, s_a2, j.at(1))
                wait(e, s_ohl, j.at(1))
                if not j.first(1):
                    wait(e, s_d4b, j.at())
                for a in range(2):
                    for s in range(4):
                        mm = e.matmul(S2[:, a * W:(a + 1) * W], BS[:, q, a, s * 128:(s + 1) * 128], ohl[:, k, s, :],
                                      start=(s == 0), stop=(s == 3))
                mm.then_inc(s_p4, 1)

            pipeline(e, T, U, D, [(5, p3), (1, p1), (6, p4), (3, p2)])


def steps(n, stages, before=None):
    for i in range(n + max(lag for lag, _ in stages)):
        if before is not None and i < n:
            before(i)
        for lag, f in stages:
            if 0 <= i - lag < n:
                f(i - lag)


def recycle(nc, used):
    with nc.Block() as blk:
        @blk.gpsimd
        def _(e):
            for s in used:
                e.sem_clear(s)
    for s in used:
        nc.release_semaphore(s)


def phase_n1(nc, d, v):
    sbt, pst = v["sbt"], v["pst"]
    used = []

    def sem(name):
        used.append(nc.alloc_semaphore(name=name))
        return used[-1]

    acc, ident, ones, dinv = v["acc"], v["ident"], v["ones"], v["dinv"]
    X1D, XS, DQ, DEG = v["X1D"], v["XS"], v["DQ"], v["DEG"]
    NG = len(GROUPS)
    with ExitStack() as ph:
        w1 = sbt(ph, "w1", [128, 13, 128])
        w2 = sbt(ph, "w2", [128, 128])
        b1 = sbt(ph, "b1", [128, 1])
        b2 = sbt(ph, "b2", [128, 1])
        xt = sbt(ph, "xt", [128, 3, 512])
        mean = sbt(ph, "mean", [128, 2, 512])
        std = sbt(ph, "std", [128, 2, 512])
        dq = sbt(ph, "dq", [128, 3, 3, 512])
        nm = sbt(ph, "nm", [NB, 4, 128])
        nt = sbt(ph, "nt", [NB, 4, 128])
        tmp = sbt(ph, "tmp1", [128, 4, 512])
        hh = sbt(ph, "hh", [128, 2, 512])
        xb = sbt(ph, "xb", [128, 2, 512])
        rr = sbt(ph, "rr", [128, 2, 512])
        x1 = sbt(ph, "x1", [128, 2, 4, 128])
        xs = sbt(ph, "xs", [128, 2, 4, 128])
        bn = sbt(ph, "bn1", [128, 4, 6])
        mv = sbt(ph, "mv1", [128, 2, 4, 2])
        vd = sbt(ph, "vd1", [128, 2, 4])
        PP = [pst(ph, f"PP{k}", [128, 512]) for k in range(3)]
        PY = pst(ph, "PY", [128, 512])
        TR = [pst(ph, f"TR{k}", [128, 512]) for k in range(2)]
        XT = pst(ph, "XT", [128, 512])
        DG = pst(ph, "DG", [128, 512])
        P1 = [PP[1], DG]
        n_w = sem("n_w")
        n_x = [sem(f"n_x{k}") for k in range(3)]
        n_dq = sem("n_dq")
        n_q = [sem(f"n_q{k}") for k in range(3)]
        s_dg = sem("n_dg")
        s_d1 = sem("n_d1")
        s_lg = sem("n_lg")
        s_nm = sem("n_nm")
        s_tq = sem("n_tq")
        s_dv = sem("n_dv")
        n_o = [sem(f"n_o{k}") for k in range(2)]
        s_var = sem("n_var")
        s_sq = sem("n_sq")
        s_a2 = sem("n_a2")
        s_b = sem("n_b")
        s_d = sem("n_d")
        s_h = sem("n_h")
        s_y = sem("n_y")
        s_e = sem("n_e")
        s_r = sem("n_r")
        s_f1 = sem("n_f1")
        s_rs = sem("n_rs")
        s_f2 = sem("n_f2")
        s_s = sem("n_s")
        s_k = sem("n_k")
        s_v = sem("n_v")
        blk = ph.enter_context(nc.Block())

        def cols(g):
            o, n = GROUPS[g]
            return slice(o, o + n), n, n // 128

        @blk.sync
        def _(e):
            e.dma_start(DEG.rearrange("(a n) -> a n", a=1), acc[0:1, 2, :]).then_inc(s_dg, 16)
            e.wait_ge(s_dg, 16)
            e.dma_start(nt[:, 0, :], DEG.rearrange("(b n) -> b n", n=128)).then_inc(s_dg, 16)
            e.dma_start(w1[:, :, :], d["w1"].rearrange("(k p) f -> p k f", p=128)).then_inc(n_w, 16)
            e.dma_start(w2[:, :], d["w2"]).then_inc(n_w, 16)
            e.dma_start(b1[:, :], d["b1"]).then_inc(n_w, 16)
            e.dma_start(b2[:, :], d["b2"]).then_inc(n_w, 16)

            def load(g):
                c, n, _ = cols(g)
                if g >= 3:
                    e.wait_ge(s_h, g - 2)
                e.dma_start(xt[:, g % 3, 0:n], d["xT"][:, c]).then_inc(n_x[g % 3], 16)
                if g >= 3:
                    e.wait_ge(s_d, g - 2)
                if g == 0:
                    e.wait_ge(s_nm, 1)
                    e.dma_start(DQ.rearrange("q (b n) -> b q n", n=128), nm[:, 0:3, :]).then_inc(n_dq, 16)
                    e.wait_ge(n_dq, 16)
                e.dma_start(dq[:, g % 3, :, 0:n], DQ[:, c].partition_broadcast(128)).then_inc(n_q[g % 3], 16)

            def store(g):
                c, n, nb = cols(g)
                e.wait_ge(s_f2, g + 1)
                for t, s in ((X1D, x1), (XS, xs)):
                    e.dma_start(t[c, :].rearrange("(b p) f -> p b f", p=128), s[:, g % 2, 0:nb, :])\
                     .then_inc(n_o[g % 2], 16)

            steps(NG, [(0, load), (5, store)])
            for k in range(2):
                e.wait_ge(n_o[k], 32 * len(range(k, NG, 2)))

        @blk.vector
        def _(e):
            ch = Chain(e, s_v)

            e.wait_ge(s_dg, 32)
            ch(e.tensor_scalar(nt[:, 1, :], nt[:, 0, :], 1.0, None, ALU.max))
            ch(e.tensor_scalar(nt[:, 2, :], nt[:, 0, :], 1.0, None, ALU.add))
            ch.raises(s_d1)
            ch(e.reciprocal(nm[:, 0, :], nt[:, 1, :]))
            e.wait_ge(s_lg, 1)
            ch(e.tensor_scalar(nm[:, 1, :], nt[:, 3, :], 1.0 / 2.5, None, ALU.mult))
            ch.sync()
            ch(e.tensor_scalar(nt[:, 1, :], nt[:, 3, :], EPS, 1.0 / 2.5, ALU.max, ALU.mult))
            ch.sync()
            ch(e.reciprocal(nt[:, 3, :], nt[:, 1, :]))
            ch.sync()
            ch(e.scalar_tensor_tensor(nm[:, 2, :], nt[:, 0, :], 1.0, nt[:, 3, :], ALU.min, ALU.mult))
            ch.raises(s_nm)
            e.wait_ge(s_lg, 2)
            ch(e.reciprocal(nm[:, 3, :], nt[:, 2, :]))
            ch.raises(s_dv)
            e.wait_ge(s_tq, 1)
            ch(e.tensor_copy(dinv[:, :], DG[:, 0:NB]))
            ch.raises(s_dv)

            def a(g):
                c, n, _ = cols(g)
                q = g % 2
                t = lambda k: tmp[:, k, 0:n]
                r = dq[:, g % 3, 0, 0:n]
                ch.sync()
                e.wait_ge(n_q[g % 3], 16 * (g // 3 + 1))
                if g >= 2:
                    e.wait_ge(s_b, g - 1)
                ch(e.tensor_tensor(mean[:, q, 0:n], acc[:, 0, c], r, ALU.mult))
                ch(e.tensor_tensor(t(0), acc[:, 1, c], r, ALU.mult))
                ch.sync()
                ch(e.tensor_tensor(t(1), mean[:, q, 0:n], mean[:, q, 0:n], ALU.mult))
                ch.sync()
                ch(e.tensor_tensor(t(0), t(0), t(1), ALU.subtract))
                ch.sync()
                ch(e.tensor_scalar(std[:, q, 0:n], t(0), 0.0, EPS, ALU.max, ALU.add))
                ch.raises(s_var)

            def a2(g):
                c, n, _ = cols(g)
                q = g % 2
                e.wait_ge(s_sq, g + 1)
                ch(e.scalar_tensor_tensor(std[:, q, 0:n], acc[:, 2, c], 1.0, std[:, q, 0:n], ALU.min, ALU.mult))
                ch.raises(s_a2)

            def dd(g):
                _, n, _ = cols(g)
                q = g % 2
                e.wait_ge(s_b, g + 1)
                ch(e.tensor_tensor(tmp[:, 2, 0:n], P1[q][:, 0:n], dq[:, g % 3, 1, 0:n], ALU.mult))
                ch(e.tensor_tensor(tmp[:, 3, 0:n], PP[2][:, 0:n], dq[:, g % 3, 2, 0:n], ALU.mult))
                ch.sync()
                ch(e.tensor_tensor(tmp[:, 2, 0:n], tmp[:, 2, 0:n], tmp[:, 3, 0:n], ALU.add))
                ch.sync()
                if g >= 2:
                    e.wait_ge(s_y, g - 1)
                ch(e.tensor_tensor(hh[:, q, 0:n], PP[0][:, 0:n], tmp[:, 2, 0:n], ALU.add))
                ch.raises(s_d)

            def ee(g):
                _, n, _ = cols(g)
                e.wait_ge(s_y, g + 1)
                e.wait_ge(s_h, g + 1)
                if g >= 2:
                    e.wait_ge(s_r, g - 1)
                ch(e.tensor_tensor(rr[:, g % 2, 0:n], PY[:, 0:n], xb[:, g % 2, 0:n], ALU.add))
                ch.raises(s_e)

            def f1(g):
                _, n, nb = cols(g)
                q = g % 2
                e.wait_ge(s_r, g + 1)
                for b in range(nb):
                    ch(e.bn_stats(bn[:, b, :], TR[q][:, b * 128:(b + 1) * 128]))
                ch.sync()
                for b in range(nb):
                    ch(e.bn_aggr(mv[:, q, b, :], bn[:, b, :]))
                ch.sync()
                ch(e.tensor_scalar(vd[:, q, 0:nb], mv[:, q, 0:nb, 1], EPS, None, ALU.add))
                ch.raises(s_f1)

            def f2(g):
                c, n, nb = cols(g)
                q = g % 2
                e.wait_ge(s_rs, g + 1)
                ch(e.reciprocal(vd[:, q, 0:nb], vd[:, q, 0:nb]))
                ch.sync()
                if g >= 2:
                    e.wait_ge(n_o[q], 32 * (g // 2))
                    e.wait_ge(s_s, g - 1)
                for b in range(nb):
                    ch(e.tensor_scalar(x1[:, q, b, :], TR[q][:, b * 128:(b + 1) * 128], mv[:, q, b, 0:1],
                                       vd[:, q, b:b + 1], ALU.subtract, ALU.mult))
                ch.sync()
                for b in range(nb):
                    o = c.start // 128 + b
                    ch(e.tensor_scalar(xs[:, q, b, :], x1[:, q, b, :], dinv[:, o:o + 1], None, ALU.mult))
                ch.raises(s_f2)

            steps(NG, [(1, a2), (2, dd), (3, ee), (4, f1), (5, f2), (0, a)])

        @blk.scalar
        def _(e):
            e.wait_ge(n_w, 64)

            e.wait_ge(s_d1, 1)
            e.activation(nt[:, 3, :], nt[:, 2, :], ACT.Ln).then_inc(s_lg, 1)
            e.wait_ge(s_lg, 1)
            e.activation(nt[:, 2, :], nt[:, 2, :], ACT.Sqrt).then_inc(s_lg, 1)

            e.wait_ge(n_w, 64)

            def roots(g):
                c, n, _ = cols(g)
                q = g % 2
                e.wait_ge(s_var, g + 1)
                e.activation(std[:, q, 0:n], std[:, q, 0:n], ACT.Sqrt).then_inc(s_sq, 1)

            def h(g):
                _, n, _ = cols(g)
                q = g % 2
                e.wait_ge(s_d, g + 1)
                e.activation(hh[:, q, 0:n], hh[:, q, 0:n], ACT.Relu, bias=b1[:, 0:1])
                e.wait_ge(n_x[g % 3], 16 * (g // 3 + 1))
                if g >= 2:
                    e.wait_ge(s_e, g - 1)
                e.activation(xb[:, q, 0:n], xt[:, g % 3, 0:n], ACT.Identity, bias=b2[:, 0:1], scale=2.0).then_inc(s_h, 1)

            def rs(g):
                nb = cols(g)[2]
                e.wait_ge(s_f1, g + 1)
                e.activation(vd[:, g % 2, 0:nb], vd[:, g % 2, 0:nb], ACT.Sqrt).then_inc(s_rs, 1)

            def k(g):
                c, n, _ = cols(g)
                e.wait_ge(s_s, g + 1)
                e.copy(acc[:, 0, c], XT[:, 0:n]).then_inc(s_k, 1)

            steps(NG, [(2, h), (4, rs), (6, k), (0, roots)])

        @blk.tensor
        def _(e):
            e.wait_ge(s_dv, 1)
            e.transpose(DG[:, 0:NB], nm[:, 3, :], ident[0:NB, 0:NB]).then_inc(s_tq, 1)
            e.wait_ge(n_w, 64)

            def y(g):
                _, n, _ = cols(g)
                e.wait_ge(s_h, g + 1)
                if g >= 1:
                    e.wait_ge(s_e, g)
                e.matmul(PY[:, 0:n], w2[:, :], hh[:, g % 2, 0:n], start=True, stop=True).then_inc(s_y, 1)

            def r(g):
                c, n, nb = cols(g)
                q = g % 2
                e.wait_ge(s_e, g + 1)
                if g >= 2:
                    e.wait_ge(s_f2, g - 1)
                for b in range(nb):
                    mm = e.transpose(TR[q][:, b * 128:(b + 1) * 128], rr[:, q, b * 128:(b + 1) * 128], ident[:, :])
                mm.then_inc(s_r, 1)

            def s(g):
                _, n, nb = cols(g)
                e.wait_ge(s_f2, g + 1)
                if g >= 1:
                    e.wait_ge(s_k, g)
                for b in range(nb):
                    mm = e.transpose(XT[:, b * 128:(b + 1) * 128], xs[:, g % 2, b, :], ident[:, :])
                mm.then_inc(s_s, 1)

            def b(g):
                c, n, _ = cols(g)
                q = g % 2
                e.wait_ge(n_x[g % 3], 16 * (g // 3 + 1))
                e.wait_ge(s_a2, g + 1)
                agg = (mean[:, q, 0:n], acc[:, 3, c], acc[:, 4, c], std[:, q, 0:n])
                if g >= 2:
                    e.wait_ge(s_d, g - 1)
                if g == 1:
                    e.wait_ge(s_dv, 2)
                for p, t in ((1, P1[q]), (2, PP[2]), (0, PP[0])):
                    if p == 2 and g >= 1:
                        e.wait_ge(s_d, g)
                    if p == 0:
                        e.matmul(t[:, 0:n], w1[:, 0, :], xt[:, g % 3, 0:n], start=True, stop=False)
                    for k in range(4):
                        mm = e.matmul(t[:, 0:n], w1[:, 1 + 4 * p + k, :], agg[k],
                                      start=(p > 0 and k == 0), stop=(k == 3))
                mm.then_inc(s_b, 1)

            steps(NG, [(3, y), (4, r), (6, s), (1, b)])
    recycle(nc, used)


def phase_gcn(nc, d, v):
    sem, sbt, pst = v["sem"], v["sbt"], v["pst"]
    acc, ident, ones, dinv = v["acc"], v["ident"], v["ones"], v["dinv"]
    baseF, tb, iotaW, XS = v["baseF"], v["tb"], v["iotaW"], v["XS"]
    TAB, ADT = v["TAB"], v["ADT"]
    NG = len(GROUPS)
    with ExitStack() as ph:
        meta = sbt(ph, "metac", [128, 4, 12], I32)
        G = sbt(ph, "Gc", [128, 4, 4, 128])
        oh = sbt(ph, "ohc", [128, 2, 4, W])
        iob = sbt(ph, "iobc", [128, 2, W])
        S = [pst(ph, f"Sc{k}", [128, 512]) for k in range(2)]
        gw = sbt(ph, "gw", [128, 128])
        gwT = sbt(ph, "gwT", [128, 2, 128])
        at = sbt(ph, "at", [128, 2, 2])
        gb = sbt(ph, "gb", [128, 3, 128])
        vv = sbt(ph, "vv", [128, 3, 2])
        tt = sbt(ph, "tt", [128, 2, 4, 128])
        zz = sbt(ph, "zz", [128, 2, 4, 128])
        ts = sbt(ph, "ts", [128, 4, 4, 130])
        adt = sbt(ph, "adt", [128, 4, 4, 2])
        bn = sbt(ph, "bn2", [128, 4, 6])
        mv = sbt(ph, "mv2", [128, 2, 4, 2])
        rs = sbt(ph, "rs2", [128, 2, 4])
        lr = sbt(ph, "lr", [1, 2, 512])
        Q = [pst(ph, f"Q{k}", [128, 512]) for k in range(2)]
        HT = pst(ph, "HT", [128, 512])
        AB = pst(ph, "AB", [128, 512])
        LR = [pst(ph, f"LR{k}", [128, 512]) for k in range(2)]
        PV = AB[:, 500:504]
        l_mt = [sem(f"c_mt{k}") for k in range(4)]
        l_g = [sem(f"c_g{k}") for k in range(4)]
        s_iob = sem("c_iob")
        s_oh = sem("c_oh")
        s_mm = sem("c_mm")
        s_acc = sem("c_acc")
        s_pool = v["s_pool"]
        s_sync = v["s_sync"]
        w = sem("m_w")
        s_o = [sem(f"m_o{k}") for k in range(4)]
        s_pv = sem("m_pv")
        s_vv = sem("m_vv")
        s_q = sem("m_q")
        s_f1 = sem("m_f1")
        s_rs = sem("m_rs")
        s_f2 = sem("m_f2")
        s_h = sem("m_h")
        s_t = sem("m_t")
        s_c1 = sem("m_c1")
        s_lr = sem("m_lr")
        s_ab = sem("m_ab")
        s_g = sem("m_g")
        s_v = sem("m_v")
        blk = ph.enter_context(nc.Block())

        def cols(g):
            o, n = GROUPS[g]
            return slice(o, o + n), n, n // 128

        def entries(e, ends, f):
            def run(g):
                if g == 0:
                    for o in range(4):
                        f(Entry(0, o))
                with e.bass.Fori(ends[g - 1] if g else 4, ends[g], 4, engines=bass.OrderedEngineSet([e.engine])) as i:
                    for o in range(4):
                        f(Entry(i, o))
            return run

        @blk.gpsimd
        def _(e):
            T = load_end(e, tb, NG - 1)

            def gather(j):
                k = j.slot(4)
                wait(e, l_mt[k], 16 * j.uses(4))
                if not j.first(4):
                    wait(e, s_mm, j.at(-3))
                e.sem_inc(s_pool, 1)
                for s in range(4):
                    e.indirect_dma_start(G[:, k, s, :], None, XS,
                                         bass.IndirectOffsetOnAxis(ap=meta[:, k, s:s + 1], axis=0)).then_inc(l_g[k], 16)

            pipeline(e, T, 4, 4, [(0, gather)])

        @blk.sync
        def _(e):
            e.dma_start(gw[:, :], d["gcnw"]).then_inc(w, 16)
            e.dma_start(gwT[:, :, :], d["gatwT"].rearrange("(h c) f -> c h f", h=2)).then_inc(w, 16)
            e.dma_start(at[:, 0, :], d["atts"]).then_inc(w, 16)
            e.dma_start(at[:, 1, :], d["attd"]).then_inc(w, 16)
            for k, t in enumerate(("gcnb", "gamma", "beta")):
                e.dma_start(gb[:, k, :], d[t].partition_broadcast(128)).then_inc(w, 16)

            T = load_end(e, tb, NG - 1)

            def load(j):
                k = j.slot(4)
                c = chunk_of(e, tb, j)
                before = 64 * j.uses(4, -1), j.at(-3)
                if not j.first(4):
                    wait_sync(e, l_g[k], before[0], s_sync)
                    wait_sync(e, s_oh, before[1], s_sync)
                e.dma_start(meta[:, k, :], d["meta"][ds(c, 1), :, :].rearrange("a p s -> (a p) s")).then_inc(l_mt[k], 16)

            pipeline(e, T, 4, 4, [(0, load)])

        @blk.tensor
        def _(e):
            e.wait_ge(w, 112)
            for h in range(2):
                for k in range(2):
                    mm = e.matmul(PV[:, 2 * k + h:2 * k + h + 1], gwT[:, h, :], at[:, k, h:h + 1], start=True, stop=True)
            mm.then_inc(s_pv, 1)

            ends = [load_end(e, tb, g) for g in range(NG)]

            def mm(j):
                k, q = j.slot(4), j.slot(2)
                wait(e, s_oh, j.at(1))
                wait(e, l_g[k], 64 * j.uses(4))
                if not j.first(2):
                    wait(e, s_acc, j.at(-1))
                for s in range(4):
                    m = e.matmul(S[q][:, 0:W], G[:, k, s, :], oh[:, q, s, :], start=(s == 0), stop=(s == 3))
                m.then_inc(s_mm, 1)

            def q(g):
                c, n, nb = cols(g)
                e.wait_ge(s_acc, ends[g])
                if g >= 2:
                    e.wait_ge(s_f1, g - 1)
                for b in range(nb):
                    mm = e.matmul(Q[g % 2][:, b * 128:(b + 1) * 128], acc[:, 0, c.start + b * 128:c.start + (b + 1) * 128],
                                  gw[:, :], start=True, stop=True)
                mm.then_inc(s_q, 1)

            def t(g):
                c, n, nb = cols(g)
                e.wait_ge(s_h, g + 1)
                if g >= 1:
                    e.wait_ge(s_c1, g)
                for b in range(nb):
                    mm = e.transpose(HT[:, b * 128:(b + 1) * 128], ts[:, g % 4, b, 0:128], ident[:, :])
                mm.then_inc(s_t, 1)

            def a(g):
                c, n, nb = cols(g)
                e.wait_ge(s_c1, g + 1)
                e.wait_ge(s_vv, 1)
                if g >= 1:
                    e.wait_ge(s_g, g)
                for b in range(nb):
                    e.matmul(AB[:, b * 4:b * 4 + 4], acc[:, 1, c.start + b * 128:c.start + (b + 1) * 128],
                             vv[:, 0:2, :].rearrange("p k h -> p (k h)"), start=True, stop=True)
                for h in range(2):
                    mm = e.matmul(LR[h][0:1, 0:n], vv[:, 2, h:h + 1], acc[:, 1, c], start=True, stop=True)
                mm.then_inc(s_ab, 1)

            steps(NG, [(0, q), (2, t), (3, a)], entries(e, ends, mm))

        @blk.vector
        def _(e):
            ch = Chain(e, s_v)
            e.wait_ge(w, 112)
            ch(e.memset(acc[32:33, 3:5, :], 1.0))
            e.wait_ge(s_pv, 1)
            ch(e.tensor_copy(vv[:, 0:2, :].rearrange("p k h -> p (k h)"), PV[:, :]))
            ch.sync()
            ch(e.tensor_tensor(vv[:, 2, :], vv[:, 0, :], vv[:, 1, :], ALU.add))
            ch.raises(s_vv)

            ends = [load_end(e, tb, g) for g in range(NG)]

            def onehot(j):
                k, q = j.slot(4), j.slot(2)
                e.tensor_scalar(iob[:, q, :], iotaW[:, :], baseF[:, ds(j.at(), 1)], None, ALU.add).then_inc(s_iob, 1)
                wait(e, l_mt[k], 16 * j.uses(4))
                if not j.first(2):
                    wait(e, s_mm, j.at(-1))
                wait(e, s_iob, j.at(1))
                e.tensor_tensor(oh[:, q, :, :], iob[:, q:q + 1, :].to_broadcast([128, 4, W]),
                                meta[:, k, 4:8].unsqueeze(2).to_broadcast([128, 4, W]),
                                ALU.is_equal).then_inc(s_oh, 1)

            def add(j):
                b = base_of(e, tb, j)
                wait(e, s_mm, j.at(1))
                if not j.first(1):
                    wait(e, s_acc, j.at())
                a = acc[:, 0, ds(b, W)]
                e.tensor_tensor(a, a, S[j.slot(2)][:, 0:W], ALU.add).then_inc(s_acc, 1)

            def entry(j):
                onehot(j)
                add(j)

            def f1(g):
                c, n, nb = cols(g)
                q = g % 2
                e.wait_ge(s_q, g + 1)
                for b in range(nb):
                    o = c.start // 128 + b
                    ch(e.scalar_tensor_tensor(tt[:, q, b, :], Q[q][:, b * 128:(b + 1) * 128], dinv[:, o:o + 1],
                                              gb[:, 0, :], ALU.mult, ALU.add))
                ch.sync()
                for b in range(nb):
                    ch(e.bn_stats(bn[:, b, :], tt[:, q, b, :]))
                ch.sync()
                for b in range(nb):
                    ch(e.bn_aggr(mv[:, q, b, :], bn[:, b, :]))
                ch.sync()
                ch(e.tensor_scalar(rs[:, q, 0:nb], mv[:, q, 0:nb, 1], EPS, None, ALU.add))
                ch.raises(s_f1)

            def f2(g):
                c, n, nb = cols(g)
                q = g % 2
                e.wait_ge(s_rs, g + 1)
                ch(e.reciprocal(rs[:, q, 0:nb], rs[:, q, 0:nb]))
                ch.sync()
                for b in range(nb):
                    ch(e.scalar_tensor_tensor(tt[:, q, b, :], tt[:, q, b, :], mv[:, q, b, 0:1], gb[:, 1, :],
                                              ALU.subtract, ALU.mult))
                ch.sync()
                if g >= 2:
                    e.wait_ge(s_h, g - 1)
                for b in range(nb):
                    ch(e.scalar_tensor_tensor(zz[:, q, b, :], tt[:, q, b, :], rs[:, q, b:b + 1], gb[:, 2, :],
                                              ALU.mult, ALU.add))
                ch.raises(s_f2)

            def gg(g):
                c, n, nb = cols(g)
                q = g % 2
                e.wait_ge(s_ab, g + 1)
                AV = AB[:, 0:4 * nb].rearrange("p (b k) -> p b k", k=4)
                q = g % 4
                if g >= 4:
                    e.wait_ge(s_o[q], 32 * (g // 4))
                ch(e.tensor_copy(ts[:, q, 0:nb, 128:130], AV[:, :, 0:2]))
                ch(e.tensor_copy(adt[:, q, 0:nb, :], AV[:, :, 2:4]))
                e.wait_ge(s_lr, g + 1)
                for h in range(2):
                    ch(e.tensor_tensor(acc[0:1, 3 + h, c], lr[0:1, h, 0:n], LR[h][0:1, 0:n], ALU.max))
                ch.raises(s_g)

            steps(NG, [(1, f2), (0, f1), (3, gg)], entries(e, ends, entry))

        @blk.scalar
        def _(e):
            def r(g):
                nb = cols(g)[2]
                e.wait_ge(s_f1, g + 1)
                e.activation(rs[:, g % 2, 0:nb], rs[:, g % 2, 0:nb], ACT.Sqrt).then_inc(s_rs, 1)

            def h(g):
                nb, q = cols(g)[2], g % 2
                e.wait_ge(s_f2, g + 1)
                if g >= 4:
                    e.wait_ge(s_o[g % 4], 32 * (g // 4))
                    e.wait_ge(s_t, g - 3)
                e.activation(ts[:, g % 4, 0:nb, 0:128], zz[:, q, 0:nb, :], ACT.Silu).then_inc(s_h, 1)

            def c1(g):
                c, n, nb = cols(g)
                e.wait_ge(s_t, g + 1)
                for h in range(2):
                    i = e.copy(acc[:, 1 + h, c], HT[:, 0:n])
                i.then_inc(s_c1, 1)

            def scaled(g):
                _, n, _ = cols(g)
                e.wait_ge(s_ab, g + 1)
                if g >= 1:
                    e.wait_ge(s_g, g)
                for h in range(2):
                    i = e.mul(lr[0:1, h, 0:n], LR[h][0:1, 0:n], 0.2)
                i.then_inc(s_lr, 1)

            def store(g):
                c, n, nb = cols(g)
                q = g % 4
                e.wait_ge(s_g, g + 1)
                e.dma_start(TAB[c, :].rearrange("(b p) f -> p b f", p=128), ts[:, q, 0:nb, :]).then_inc(s_o[q], 16)
                e.dma_start(ADT[c, :].rearrange("(b p) f -> p b f", p=128), adt[:, q, 0:nb, :]).then_inc(s_o[q], 16)

            steps(NG, [(4, store), (2, c1), (1, h), (0, r), (3, scaled)])
            for k in range(4):
                e.wait_ge(s_o[k], 32 * len(range(k, NG, 4)))


def phase_gat(nc, d, v):
    sem, sbt, pst = v["sem"], v["sbt"], v["pst"]
    acc, baseF, tb, iotaW = v["acc"], v["baseF"], v["tb"], v["iotaW"]
    ident, ones, TAB, ADT = v["ident"], v["ones"], v["TAB"], v["ADT"]
    with ExitStack() as ph:
        meta = sbt(ph, "metat", [128, 8, 12], I32)
        G = sbt(ph, "Gt", [128, 8, 4, 130])
        ad = sbt(ph, "ad", [128, 8, 1])
        iob = sbt(ph, "iobt", [128, 2, W])
        neq = sbt(ph, "neqt", [128, 2, 4, W])
        M = sbt(ph, "M", [128, 2, 4, 2, W])
        TE = sbt(ph, "TE", [128, 2, CH])
        EX = sbt(ph, "EX", [128, 2, CH])
        P = sbt(ph, "P", [128, 2, CH])
        lt = sbt(ph, "lt", [128, 2, 3])
        ln = sbt(ph, "ln", [1, 2, 2, W])
        df = sbt(ph, "df", [1, 2, 2, W])
        sc = sbt(ph, "sc", [1, 4, 2 * W])
        nl = sbt(ph, "nl", [128, 2, 1])
        dsum = sbt(ph, "dsum", [128, 4, 1])
        neg = sbt(ph, "neg", [1, 1])
        MT = [pst(ph, f"MT{k}", [128, CH]) for k in range(2)]
        LT = pst(ph, "LT", [128, 512])
        NL = pst(ph, "NL", [128, 512])
        PT = [pst(ph, f"PT{k}", [128, CH]) for k in range(2)]
        SR = [pst(ph, f"SR{k}", [128, 512]) for k in range(2)]
        l_mt = [sem(f"g_mt{k}") for k in range(8)]
        l_g = [sem(f"g_g{k}") for k in range(8)]
        s_iob = sem("g_iob")
        s_nq = sem("g_nq")
        s_m = sem("g_m")
        s_t1 = sem("g_t1")
        s_mx = sem("g_mx")
        s_lt0 = sem("g_lt0")
        s_lt = sem("g_lt")
        s_a1 = sem("g_a1")
        s_t2 = sem("g_t2")
        s_ln = sem("g_ln")
        s_df = sem("g_df")
        s_st = sem("g_st")
        s_lk = sem("g_lk")
        s_sc = sem("g_sc")
        s_t3 = sem("g_t3")
        s_nl = sem("g_nl")
        s_ex = sem("g_ex")
        s_t4 = sem("g_t4")
        s_p = sem("g_p")
        s_t5 = sem("g_t5")
        s_u1 = sem("g_u1")
        s_u = sem("g_u")
        s_i = sem("g_i")
        s_pool = v["s_pool"]
        s_sync = v["s_sync"]
        blk = ph.enter_context(nc.Block())
        U, D = 8, 8

        @blk.sync
        def _(e):
            T = load_T(e, tb, 1)

            def load(j):
                k = j.slot(8)
                c, b = chunk_of(e, tb, j), base_of(e, tb, j)
                before = 64 * j.uses(8, -1), j.at(-7)
                if not j.first(8):
                    wait_sync(e, l_g[k], before[0], s_sync)
                    for s in (s_nq, s_a1, s_lt0):
                        wait_sync(e, s, before[1], s_sync)
                e.dma_start(meta[:, k, :], d["meta"][ds(c, 1), :, :].rearrange("a p s -> (a p) s")).then_inc(l_mt[k], 16)
                for h in range(2):
                    e.dma_start(ad[h * W:(h + 1) * W, k, :], ADT[ds(b, W), h:h + 1],
                                allow_slow_non_contiguous=True).then_inc(l_mt[k], 16)

            pipeline(e, T, U, D, [(0, load)])

        @blk.gpsimd
        def _(e):
            T = load_T(e, tb, 1)

            def gather(j):
                k = j.slot(8)
                wait(e, l_mt[k], 48 * j.uses(8))
                if not j.first(8):
                    wait(e, s_t5, j.at(-7))
                e.sem_inc(s_pool, 1)
                for s in range(4):
                    e.indirect_dma_start(G[:, k, s, :], None, TAB,
                                         bass.IndirectOffsetOnAxis(ap=meta[:, k, s:s + 1], axis=0)).then_inc(l_g[k], 16)

            pipeline(e, T, U, D, [(0, gather)])

        @blk.vector
        def _(e):
            e.memset(neg[:, :], -1.0).then_inc(s_i, 1)
            T = load_T(e, tb, 1)
            base = {}
            regs = [e.alloc_register(f"g_base{k}") for k in range(8)]
            L = lambda b: acc[0:1, 3:5, ds(b, W)]
            UD = lambda b: ((slice(0, 128), acc[:, 1:3, ds(b, W)], 0), (slice(32, 33), acc[32:33, 3:5, ds(b, W)], 4 * W))
            sr = lambda j, p, o: SR[j.slot(2)][p, o:o + 2 * W].rearrange("p (h n) -> p h n", h=2)

            def window(j):
                q = j.slot(2)
                if not j.first(2):
                    wait(e, s_nq, j.at(-1))
                e.tensor_scalar(iob[:, q, :], iotaW[:, :], baseF[:, ds(j.at(), 1)], None, ALU.add).then_inc(s_iob, 1)

            def outside(j):
                k, q = j.slot(8), j.slot(2)
                wait(e, l_mt[k], 48 * j.uses(8))
                wait(e, s_iob, j.at(1))
                if not j.first(2):
                    wait(e, s_m, j.at(-1))
                e.tensor_tensor(neq[:, q, :, :], iob[:, q:q + 1, :].to_broadcast([128, 4, W]),
                                meta[:, k, 4:8].unsqueeze(2).to_broadcast([128, 4, W]),
                                ALU.not_equal).then_inc(s_nq, 1)

            def masked(j):
                k, q = j.slot(8), j.slot(2)
                wait(e, l_g[k], 64 * j.uses(8))
                wait(e, s_nq, j.at(1))
                if not j.first(2):
                    wait(e, s_t1, j.at(-1))
                for h in range(2):
                    i = e.scalar_tensor_tensor(M[:, q, :, h, :], neq[:, q, :, :], -BIG,
                                               G[:, k, :, 128 + h:129 + h].to_broadcast([128, 4, W]),
                                               ALU.mult, ALU.add)
                i.then_inc(s_m, 1)

            def highest(j):
                q = j.slot(2)
                wait(e, s_t1, j.at(1))
                e.tensor_reduce(lt[:, q, 0:1], MT[q][:, :], mybir.AxisListType.X, ALU.max).then_inc(s_mx, 1)

            def score(j):
                k, q = j.slot(8), j.slot(2)
                wait(e, l_mt[k], 48 * j.uses(8))
                wait(e, s_mx, j.at(1))
                e.tensor_tensor(lt[:, q, 1:2], lt[:, q, 0:1], ad[:, k, :], ALU.add).then_inc(s_lt0, 1)

            def leak_score(j):
                q = j.slot(2)
                if not j.first(2):
                    wait(e, s_t2, j.at(-1))
                wait(e, s_lt0, j.at(1))
                e.scalar_tensor_tensor(lt[:, q, 2:3], lt[:, q, 1:2], 0.2, lt[:, q, 1:2], ALU.mult, ALU.max).then_inc(s_lt, 1)

            def new_max(j):
                q = j.slot(2)
                base[0] = keep(e, regs, j, base_of(e, tb, j))
                wait(e, s_t2, j.at(1))
                if not j.first(2):
                    wait(e, s_t3, j.at(-1))
                    wait(e, s_st, j.at(-1))
                if not j.first(1):
                    wait(e, s_st, j.at())
                e.tensor_tensor(ln[:, q, :, :], L(base[0]), LT[0:1, 0:2 * W].rearrange("p (h n) -> p h n", h=2), ALU.max)\
                 .then_inc(s_ln, 1)

            def step_max(j):
                q = j.slot(2)
                if not j.first(2):
                    wait(e, s_sc, j.at(-1))
                wait(e, s_ln, j.at(1))
                e.tensor_tensor(df[:, q, :, :], L(base[0]), ln[:, q, :, :], ALU.subtract).then_inc(s_df, 1)

            def leak(j):
                q = j.slot(2)
                wait(e, s_a1, j.at(1))
                e.scalar_tensor_tensor(TE[:, q, :], TE[:, q, :], 0.2, TE[:, q, :], ALU.mult, ALU.max).then_inc(s_lk, 1)

            def rescale(j):
                base[1] = kept(e, regs, j)
                wait(e, s_t5, j.at(1))
                if not j.first(1):
                    wait(e, s_u, j.at())
                for p, a, o in UD(base[1]):
                    i = e.tensor_tensor(a, a, sr(j, p, 2 * W), ALU.mult)
                i.then_inc(s_u1, 1)

            def add(j):
                wait(e, s_u1, j.at(1))
                for p, a, o in UD(base[1]):
                    i = e.tensor_tensor(a, a, sr(j, p, o), ALU.add)
                i.then_inc(s_u, 1)

            pipeline(e, T, U, D, [(6, rescale), (3, new_max), (1, window), (3, step_max), (6, add),
                                  (2, highest), (1, outside), (2, score), (1, masked), (2, leak_score), (3, leak)])

        @blk.scalar
        def _(e):
            T = load_T(e, tb, 1)

            def a1(j):
                k, q = j.slot(8), j.slot(2)
                wait(e, s_mx, j.at(1))
                wait(e, l_mt[k], 48 * j.uses(8))
                if not j.first(2):
                    wait(e, s_ex, j.at(-1))
                e.activation(TE[:, q, :], MT[q][:, :], ACT.Identity, bias=ad[:, k, 0:1]).then_inc(s_a1, 1)

            def a2(j):
                wait(e, s_df, j.at(1))
                if not j.first(4):
                    wait(e, s_t5, j.at(-3))
                e.activation(sc[:, j.slot(4), :], df[:, j.slot(2), :, :].rearrange("p h n -> p (h n)"), ACT.Exp).then_inc(s_sc, 1)

            def keep_max(j):
                b = base_of(e, tb, j)
                wait(e, s_df, j.at(1))
                e.copy(acc[0:1, 3:5, ds(b, W)], ln[:, j.slot(2), :, :]).then_inc(s_st, 1)

            def a3(j):
                q = j.slot(2)
                wait(e, s_t3, j.at(1))
                e.copy(nl[:, q, :], NL[:, 0:1]).then_inc(s_nl, 1)
                wait(e, s_lk, j.at(1))
                if not j.first(2):
                    wait(e, s_t4, j.at(-1))
                if not j.first(4):
                    wait(e, s_t5, j.at(-3))
                wait(e, s_nl, j.at(1))
                e.activation(EX[:, q, :], TE[:, q, :], ACT.Exp, bias=nl[:, q, 0:1],
                             accum_out=dsum[:, j.slot(4), :]).then_inc(s_ex, 1)

            def a4(j):
                q = j.slot(2)
                wait(e, s_t4, j.at(1))
                if not j.first(2):
                    wait(e, s_t5, j.at(-1))
                e.copy(P[:, q, :], PT[q][:, :]).then_inc(s_p, 1)

            pipeline(e, T, U, D, [(5, a4), (4, a3), (3, a2), (3, keep_max), (2, a1)])

        @blk.tensor
        def _(e):
            e.wait_ge(s_i, 1)
            T = load_T(e, tb, 1)

            def t1(j):
                q = j.slot(2)
                wait(e, s_m, j.at(1))
                if not j.first(2):
                    wait(e, s_a1, j.at(-1))
                for s in range(4):
                    m = e.transpose(MT[q][:, s * 128:(s + 1) * 128],
                                    M[:, q, s, :, :].rearrange("p h n -> p (h n)"), ident[:, :])
                m.then_inc(s_t1, 1)

            def t2(j):
                wait(e, s_lt, j.at(1))
                if not j.first(1):
                    wait(e, s_ln, j.at())
                e.transpose(LT[0:1, 0:2 * W], lt[:, j.slot(2), 2:3], ident[:, :]).then_inc(s_t2, 1)

            def t3(j):
                wait(e, s_ln, j.at(1))
                if not j.first(1):
                    wait(e, s_nl, j.at())
                e.matmul(NL[:, 0:1], ln[:, j.slot(2), :, :].rearrange("p h n -> p (h n)"), neg[:, :],
                         start=True, stop=True).then_inc(s_t3, 1)

            def t4(j):
                q = j.slot(2)
                wait(e, s_ex, j.at(1))
                if not j.first(2):
                    wait(e, s_p, j.at(-1))
                for s in range(4):
                    m = e.transpose(PT[q][:, s * 128:(s + 1) * 128], EX[:, q, s * 128:(s + 1) * 128], ident[:, :])
                m.then_inc(s_t4, 1)

            def t5(j):
                k, q = j.slot(8), j.slot(2)
                wait(e, s_p, j.at(1))
                wait(e, s_sc, j.at(1))
                if not j.first(2):
                    wait(e, s_u, j.at(-1))
                e.matmul(SR[q][:, 2 * W:4 * W], ones[0:1, :], sc[:, j.slot(4), :], start=True, stop=True)
                e.matmul(SR[q][0:64, 4 * W:6 * W], dsum[:, j.slot(4), :].to_broadcast([128, 64]), ident[:, :],
                         start=True, stop=True)
                for s in range(4):
                    m = e.matmul(SR[q][:, 0:2 * W], G[:, k, s, 0:128], P[:, q, s * 128:(s + 1) * 128],
                                 start=(s == 0), stop=(s == 3))
                m.then_inc(s_t5, 1)

            pipeline(e, T, U, D, [(5, t5), (4, t4), (3, t3), (2, t2), (1, t1)])


def phase_n3(nc, d, v, out):
    sem, sbt, pst = v["sem"], v["sbt"], v["pst"]
    acc, ident, X1D = v["acc"], v["ident"], v["X1D"]
    NG, NB, R = len(GROUPS), NP // 128, 3
    with ExitStack() as ph:
        gw = sbt(ph, "gw3", [128, 256])
        gb = sbt(ph, "gb3", [128, 3, 128])
        x1 = sbt(ph, "x13", [128, R, 4, 128])
        tt = sbt(ph, "tt3", [128, R, 4, 128])
        tu = sbt(ph, "tu3", [128, R, 4, 128])
        zz = sbt(ph, "zz3", [128, R, 4, 128])
        yy = sbt(ph, "yy3", [128, R, 4, 128])
        oo = sbt(ph, "oo3", [128, R, 4, 128])
        dt = sbt(ph, "dt3", [2 * NB, 128])
        rd = sbt(ph, "rd", [128, 2 * NB])
        bn = sbt(ph, "bn3", [128, 4, 6])
        mv = sbt(ph, "mv3", [128, 2, R, 4, 2])
        rs = sbt(ph, "rs3", [128, 2, R, 4])
        nm = sbt(ph, "nm3", [128, R, 4])
        H = [[pst(ph, f"H{h}{k}", [128, 512]) for k in range(2)] for h in range(2)]
        DN = pst(ph, "DN", [128, 512])
        w = sem("o_w")
        s_den = sem("o_dn")
        s_td = sem("o_td")
        s_rd = sem("o_rd")
        s_x = [sem(f"o_x{k}") for k in range(R)]
        s_o = [sem(f"o_o{k}") for k in range(R)]
        s_mm = sem("o_mm")
        s_t = sem("o_t")
        s_a = sem("o_a")
        s_p = sem("o_p")
        s_f = [sem("o_f0"), sem("o_f1")]
        s_rs = [sem("o_r0"), sem("o_r1")]
        s_z = sem("o_z")
        s_h = sem("o_h")
        s_y = sem("o_y")
        s_n = sem("o_n")
        s_out = sem("o_out")
        s_v = sem("o_v")
        blk = ph.enter_context(nc.Block())

        def cols(g):
            o, n = GROUPS[g]
            return slice(o, o + n), n, n // 128

        def scale(g, h, b):
            col = h * NB + GROUPS[g][0] // 128 + b
            return rd[:, col:col + 1]

        @blk.sync
        def _(e):
            for h in range(2):
                e.dma_start(dt[h * NB:(h + 1) * NB, :], acc[32:33, 3 + h, :].rearrange("o (b p) -> o b p", p=128)).then_inc(s_den, 16)
            e.dma_start(gw[:, :], d["gatw"]).then_inc(w, 16)
            for k, t in enumerate(("gatb", "gamma", "beta")):
                e.dma_start(gb[:, k, :], d[t].partition_broadcast(128)).then_inc(w, 16)

            def load(g):
                c, n, nb = cols(g)
                if g >= R:
                    e.wait_ge(s_y, g - R + 1)
                e.dma_start(x1[:, g % R, 0:nb, :], X1D[c, :].rearrange("(b p) f -> p b f", p=128)).then_inc(s_x[g % R], 16)

            def store(g):
                c, n, nb = cols(g)
                q = g % R
                e.wait_ge(s_out, g + 1)
                full = (min(c.stop, N) - c.start) // 128
                if full:
                    e.dma_start(out[c.start:c.start + full * 128, :].rearrange("(b p) f -> p b f", p=128),
                                oo[:, q, 0:full, :]).then_inc(s_o[q], 16)
                else:
                    e.dma_start(out[c.start:N, :], oo[0:N - c.start, q, 0, :]).then_inc(s_o[q], 16)

            steps(NG, [(0, load), (4, store)])
            for k in range(R):
                e.wait_ge(s_o[k], 16 * len(range(k, NG, R)))

        @blk.tensor
        def _(e):
            e.wait_ge(s_den, 32)
            e.transpose(DN[:, 0:2 * NB], dt[:, :], ident[0:2 * NB, 0:2 * NB]).then_inc(s_td, 1)
            e.wait_ge(w, 64)

            def mm(g):
                c, n, nb = cols(g)
                q = g % 2
                if g >= 2:
                    e.wait_ge(s_t, g - 1)
                    e.wait_ge(s_a, g - 1)
                for b in range(nb):
                    cc = slice(c.start + b * 128, c.start + (b + 1) * 128)
                    for h in range(2):
                        m = e.matmul(H[h][q][:, b * 128:(b + 1) * 128], acc[:, 1 + h, cc], gw[:, h * 128:(h + 1) * 128],
                                     start=True, stop=True)
                m.then_inc(s_mm, 1)

            steps(NG, [(0, mm)])

        @blk.vector
        def _(e):
            ch = Chain(e, s_v)
            e.wait_ge(s_td, 1)
            ch(e.tensor_scalar(rd[:, :], DN[:, 0:2 * NB], 2.0, None, ALU.mult))
            ch.sync()
            ch(e.reciprocal(rd[:, :], rd[:, :]))
            ch.raises(s_rd)
            e.wait_ge(w, 64)

            def stats(g, k, src):
                nb, q = cols(g)[2], g % R
                for b in range(nb):
                    ch(e.bn_stats(bn[:, b, :], src[:, q, b, :]))
                ch.sync()
                for b in range(nb):
                    ch(e.bn_aggr(mv[:, k, q, b, :], bn[:, b, :]))
                ch.sync()
                ch(e.tensor_scalar(rs[:, k, q, 0:nb], mv[:, k, q, 0:nb, 1], EPS, None, ALU.add))
                ch.raises(s_f[k])

            def inverse(g, k):
                nb, q = cols(g)[2], g % R
                e.wait_ge(s_rs[k], g + 1)
                ch(e.reciprocal(rs[:, k, q, 0:nb], rs[:, k, q, 0:nb]))
                ch.sync()

            def head0(g):
                nb, q = cols(g)[2], g % R
                e.wait_ge(s_mm, g + 1)
                for b in range(nb):
                    ch(e.scalar_tensor_tensor(tt[:, q, b, :], H[0][g % 2][:, b * 128:(b + 1) * 128],
                                              scale(g, 0, b), gb[:, 0, :], ALU.mult, ALU.add))
                ch.raises(s_t)

            def stats0(g):
                e.wait_ge(s_p, g + 1)
                stats(g, 0, tt)

            def norm0(g):
                nb, q = cols(g)[2], g % R
                inverse(g, 0)
                for b in range(nb):
                    ch(e.scalar_tensor_tensor(tt[:, q, b, :], tt[:, q, b, :], mv[:, 0, q, b, 0:1], gb[:, 1, :],
                                              ALU.subtract, ALU.mult))
                ch.sync()
                for b in range(nb):
                    ch(e.scalar_tensor_tensor(zz[:, q, b, :], tt[:, q, b, :], rs[:, 0, q, b:b + 1], gb[:, 2, :],
                                              ALU.mult, ALU.add))
                ch.raises(s_z)

            def stats1(g):
                e.wait_ge(s_y, g + 1)
                if g >= R:
                    e.wait_ge(s_out, g - R + 1)
                stats(g, 1, yy)

            def shift(g):
                nb, q = cols(g)[2], g % R
                inverse(g, 1)
                ch(e.scalar_tensor_tensor(nm[:, q, 0:nb], mv[:, 1, q, 0:nb, 0], -1.0, rs[:, 1, q, 0:nb], ALU.mult, ALU.mult))
                ch.raises(s_n)

            steps(NG, [(0, head0), (4, shift), (2, norm0), (1, stats0), (3, stats1)])

        @blk.gpsimd
        def _(e):
            def mean(g):
                nb, q = cols(g)[2], g % R
                e.wait_ge(s_t, g + 1)
                e.wait_ge(s_a, g + 1)
                e.tensor_tensor(tt[:, q, 0:nb, :], tt[:, q, 0:nb, :], tu[:, q, 0:nb, :], ALU.add).then_inc(s_p, 1)

            def residual(g):
                nb, q = cols(g)[2], g % R
                e.wait_ge(s_h, g + 1)
                e.wait_ge(s_x[q], 16 * (g // R + 1))
                if g >= R:
                    e.wait_ge(s_out, g - R + 1)
                e.tensor_tensor(yy[:, q, 0:nb, :], zz[:, q, 0:nb, :], x1[:, q, 0:nb, :], ALU.add).then_inc(s_y, 1)

            steps(NG, [(0, mean), (2, residual)])

        @blk.scalar
        def _(e):
            e.wait_ge(s_rd, 1)

            def head1(g):
                nb, q = cols(g)[2], g % R
                e.wait_ge(s_mm, g + 1)
                if g >= R:
                    e.wait_ge(s_p, g - R + 1)
                for b in range(nb):
                    m = e.activation(tu[:, q, b, :], H[1][g % 2][:, b * 128:(b + 1) * 128], ACT.Identity, scale=scale(g, 1, b))
                m.then_inc(s_a, 1)

            def root(k):
                def f(g):
                    nb, q = cols(g)[2], g % R
                    e.wait_ge(s_f[k], g + 1)
                    e.activation(rs[:, k, q, 0:nb], rs[:, k, q, 0:nb], ACT.Sqrt).then_inc(s_rs[k], 1)
                return f

            def silu(g):
                nb, q = cols(g)[2], g % R
                e.wait_ge(s_z, g + 1)
                e.activation(zz[:, q, 0:nb, :], zz[:, q, 0:nb, :], ACT.Silu).then_inc(s_h, 1)

            def last(g):
                nb, q = cols(g)[2], g % R
                e.wait_ge(s_n, g + 1)
                if g >= R:
                    e.wait_ge(s_o[q], 16 * (g // R))
                for b in range(nb):
                    m = e.activation(oo[:, q, b, :], yy[:, q, b, :], ACT.Identity, bias=nm[:, q, b:b + 1],
                                     scale=rs[:, 1, q, b:b + 1])
                m.then_inc(s_out, 1)

            steps(NG, [(0, head1), (4, last), (2, silu), (1, root(0)), (3, root(1))])


def lay_out(x, src, dst, edge_attr_64, np):
    pad = EP - E
    src = np.concatenate([np.asarray(src), np.zeros(pad, np.int32)])
    dst = np.concatenate([np.asarray(dst), np.full(pad, N, np.int32)])
    minus = np.full(1, -1, np.int32)
    lin = np.concatenate([minus, dst, minus])
    chunks = lambda a: a.reshape(NCH, 4, 128)
    a = {
        "xT": np.concatenate([np.asarray(x).T, np.zeros((128, NP - N), np.float32)], axis=1),
        "lin": lin,
        "meta": np.concatenate([chunks(x).transpose(0, 2, 1) for x in (src, dst, lin[2:])], axis=2),
        "eft": np.concatenate([np.asarray(edge_attr_64).T, np.zeros((64, pad), np.float32)], axis=1),
    }
    return a


def arrays_of(np, i):
    a = lay_out(i["x"], i["src"], i["dst"], i["edge_attr_64"], np)
    g = lambda n: np.asarray(i[n])
    a["wpre"] = g("L0_gnn_W_pre")
    a["bpre"] = g("L0_gnn_b_pre")
    a["w1"] = g("L0_gnn_W_post1")
    a["b1"] = g("L0_gnn_b_post1").reshape(128, 1)
    a["w2"] = g("L0_gnn_W_post2")
    a["b2"] = g("L0_gnn_b_post2").reshape(128, 1)
    a["gcnw"] = g("L1_gnn_gcn_w")
    a["gcnb"] = g("L1_gnn_gcn_b")
    a["gatw"] = g("L1_gnn_gat_w")
    a["gatwT"] = g("L1_gnn_gat_w").T
    a["atts"] = g("L1_gnn_att_src").T
    a["attd"] = g("L1_gnn_att_dst").T
    a["gatb"] = g("L1_gnn_gat_b")
    a["gamma"] = g("L1_gnn_ln_gamma")
    a["beta"] = g("L1_gnn_ln_beta")
    return {k: np.ascontiguousarray(x) for k, x in a.items()}


def make(nc, arrays, upto=99):
    d = {k: nc.dram_tensor("in_" + k, x.shape, mybir.dt.from_np(x.dtype), kind="ExternalInput").ap()
         for k, x in arrays.items()}
    out = nc.dram_tensor("out_0_dram", (N, 128), F32, kind="ExternalOutput").ap()
    build(nc, d, out, upto)


def kernel(**inputs):
    import numpy as np
    import concourse.bacc as bacc
    from concourse.bass_utils import run_bass_kernel_spmd as run

    arrays = arrays_of(np, inputs)
    nc = bacc.Bacc("TRN2", target_bir_lowering=False, num_devices=1)
    make(nc, arrays)
    r = run(nc, [{"in_" + k: x for k, x in arrays.items()}], core_ids=[0])
    return r.results[0]["out_0_dram"]
```
